# Optimizing a Trainium2 kernel written in Bass

```python
import numpy as np
import jax
import jax.numpy as jnp

def _softmax(x, axis=-1):
    return jax.nn.softmax(x, axis=axis)

def _gelu(x):
    return jax.nn.gelu(x, approximate=True)

def _silu(x):
    return jax.nn.silu(x)

def _sigmoid(x):
    return jax.nn.sigmoid(x)

def _layernorm(x, axis=-1, eps=1e-05):
    m = jnp.mean(x, axis=axis, keepdims=True)
    v = jnp.var(x, axis=axis, keepdims=True)
    return (x - m) / jnp.sqrt(v + eps)

def _scatter_add(tgt, idx, src, axis=0):
    return tgt.at[idx].add(src)

def _segment_sum(src, seg, n):
    return jax.ops.segment_sum(src, seg, n)
kernel_name = 'mk_xattn_ffn_d2_seqx_r8_9555c8'

def setup_inputs(seed: int=0):
    np.random.seed(seed)
    _w = jnp.asarray

    def _rec_inputs():
        import jax
        import jax.numpy as jnp
        _rk = jax.random.key(seed)
        x = -0.0003929 + 0.9999 * jax.random.normal(jax.random.fold_in(_rk, 1), (16, 128, 128), jnp.float32)
        _lenS = 128 - jax.random.randint(jax.random.fold_in(_rk, 7), (16,), 0, max(1, 128 // 4) + 1, jnp.int32)
        _lenS2 = 77 - jax.random.randint(jax.random.fold_in(_rk, 8), (16,), 0, max(1, 77 // 4) + 1, jnp.int32)
        _ctx_1024P = jax.random.normal(jax.random.fold_in(_rk, 11), (16, 16, 128), jnp.float32)
        _ctx_1024c = jax.random.dirichlet(jax.random.fold_in(_rk, 511), 0.3 * jnp.ones((16,), jnp.float32), (16, 77))
        _ctx_1024t = jnp.einsum('bsk,bkd->bsd', _ctx_1024c, _ctx_1024P)
        _ctx_1024t = _ctx_1024t * jax.lax.rsqrt(jnp.mean(jnp.square(_ctx_1024t)) + 1e-12) * 0.953939
        ctx_1024 = 4.13588e-05 + 0.999923 * (_ctx_1024t + 0.3 * jax.random.normal(jax.random.fold_in(_rk, 611), (16, 77, 128), jnp.float32))
        return (x, ctx_1024)
    x, ctx_1024 = _rec_inputs()

    def _L0_xattn_setup():
        import jax, jax.numpy as jnp
        import numpy as np
        key = jax.random.key(seed)
        k1, k2 = jax.random.split(key)
        B, L, V, D = (8, 256, 128, 128)
        hidden_states = jax.random.normal(k1, (B, L, D), dtype=jnp.float32)
        visual_hidden_state = jax.random.normal(k2, (B, V, D), dtype=jnp.float32)
        return {'hidden_states': hidden_states, 'visual_hidden_state': visual_hidden_state}
    _L0_xattn_all = _L0_xattn_setup()
    _L0_xattn_in = {k: v for k, v in _L0_xattn_all.items() if k in ()}
    del _L0_xattn_all

    def _L0_ffn_setup():
        import jax, jax.numpy as jnp
        import numpy as np
        N_HEADS = 16
        NUM_EXPERTS = 4
        TOP_K = 2
        D_MODEL = 128
        GATE_HID = 128
        key = jax.random.key(seed)
        ks = jax.random.split(key, 12)
        B, T, C, E = (2, 128, D_MODEL, NUM_EXPERTS)
        s = 1.0 / np.sqrt(C)
        return {'hidden_states': jax.random.normal(ks[0], (B, T, C), jnp.float32), 'Wq': jax.random.normal(ks[1], (E, C, C), jnp.float32) * s, 'bq': jnp.zeros((E, C), jnp.float32), 'Wk': jax.random.normal(ks[2], (E, C, C), jnp.float32) * s, 'bk': jnp.zeros((E, C), jnp.float32), 'Wv': jax.random.normal(ks[3], (E, C, C), jnp.float32) * s, 'bv': jnp.zeros((E, C), jnp.float32), 'Wg1': jax.random.normal(ks[4], (C, GATE_HID), jnp.float32) * s, 'bg1': jnp.zeros((GATE_HID,), jnp.float32), 'Wg2': jax.random.normal(ks[5], (GATE_HID, E), jnp.float32) / np.sqrt(GATE_HID), 'bg2': jnp.zeros((E,), jnp.float32), 'Wo': jax.random.normal(ks[6], (C, C), jnp.float32) * s, 'bo': jnp.zeros((C,), jnp.float32)}
    _L0_ffn_all = _L0_ffn_setup()
    _L0_ffn_in = {k: v for k, v in _L0_ffn_all.items() if k in ('Wq', 'bq', 'Wk', 'bk', 'Wv', 'bv', 'Wg1', 'bg1', 'Wg2', 'bg2', 'Wo', 'bo')}
    del _L0_ffn_all

    def _L1_xattn_setup():
        import jax, jax.numpy as jnp
        import numpy as np
        DIM = 128
        NUM_HEADS = 16
        HEAD_DIM = DIM // NUM_HEADS
        ROPE_BASE = 10000.0
        SCALE = 1.0 / np.sqrt(HEAD_DIM)

        def _rotate_half(x):
            x1, x2 = jnp.split(x, 2, axis=-1)
            return jnp.concatenate([-x2, x1], axis=-1)

        def _rope(x, seq_len):
            inv_freq = 1.0 / ROPE_BASE ** (jnp.arange(0, HEAD_DIM, 2, dtype=jnp.float32) / HEAD_DIM)
            t = jnp.arange(seq_len, dtype=jnp.float32)
            freqs = jnp.outer(t, inv_freq)
            emb = jnp.concatenate([freqs, freqs], -1)
            cos = jnp.cos(emb)[None, None]
            sin = jnp.sin(emb)[None, None]
            return x * cos + _rotate_half(x) * sin
        key = jax.random.key(seed)
        ks = jax.random.split(key, 6)
        B, T_q, T_k = (4, 128, 512)
        s = 1.0 / np.sqrt(DIM)
        return {'x_query': jax.random.normal(ks[0], (B, T_q, DIM), jnp.float32), 'x_kv': jax.random.normal(ks[1], (B, T_k, DIM), jnp.float32), 'Wq': jax.random.normal(ks[2], (DIM, DIM), jnp.float32) * s, 'Wk': jax.random.normal(ks[3], (DIM, DIM), jnp.float32) * s, 'Wv': jax.random.normal(ks[4], (DIM, DIM), jnp.float32) * s, 'Wo': jax.random.normal(ks[5], (DIM, DIM), jnp.float32) * s}
    _L1_xattn_all = _L1_xattn_setup()
    _L1_xattn_in = {k: v for k, v in _L1_xattn_all.items() if k in ('Wq', 'Wk', 'Wv', 'Wo')}
    del _L1_xattn_all

    def _L1_ffn_setup():
        import jax, jax.numpy as jnp
        import numpy as np
        B, T, D, H, E, K = (2, 128, 128, 16, 8, 2)
        HS = D // H
        FF = 4 * D

        def layernorm(x, g, b, eps=1e-05):
            m = jnp.mean(x, axis=-1, keepdims=True)
            v = jnp.mean((x - m) ** 2, axis=-1, keepdims=True)
            return (x - m) * jax.lax.rsqrt(v + eps) * g + b
        key = jax.random.key(seed)
        ks = jax.random.split(key, 10)
        s = 0.02
        return {'x': jax.random.normal(ks[0], (B, T, D), jnp.float32), 'Wq': jax.random.normal(ks[1], (H, D, HS), jnp.float32) * s, 'Wk': jax.random.normal(ks[2], (H, D, HS), jnp.float32) * s, 'Wv': jax.random.normal(ks[3], (H, D, HS), jnp.float32) * s, 'gate_W': jax.random.normal(ks[4], (D, E), jnp.float32) * s, 'W1': jax.random.normal(ks[5], (E, D, FF), jnp.float32) * s, 'b1': jnp.zeros((E, FF), jnp.float32), 'W2': jax.random.normal(ks[6], (E, FF, D), jnp.float32) * s, 'b2': jnp.zeros((E, D), jnp.float32), 'ln1_g': jnp.ones((D,), jnp.float32), 'ln1_b': jnp.zeros((D,), jnp.float32), 'ln2_g': jnp.ones((D,), jnp.float32), 'ln2_b': jnp.zeros((D,), jnp.float32)}
    _L1_ffn_all = _L1_ffn_setup()
    _L1_ffn_in = {k: v for k, v in _L1_ffn_all.items() if k in ('Wq', 'Wk', 'Wv', 'gate_W', 'W1', 'b1', 'W2', 'b2', 'ln1_g', 'ln1_b', 'ln2_g', 'ln2_b')}
    del _L1_ffn_all
    return {'x': x, 'ctx_1024': ctx_1024, 'L0_ffn_Wq': _L0_ffn_in['Wq'], 'L0_ffn_bq': _L0_ffn_in['bq'], 'L0_ffn_Wk': _L0_ffn_in['Wk'], 'L0_ffn_bk': _L0_ffn_in['bk'], 'L0_ffn_Wv': _L0_ffn_in['Wv'], 'L0_ffn_bv': _L0_ffn_in['bv'], 'L0_ffn_Wg1': _L0_ffn_in['Wg1'], 'L0_ffn_bg1': _L0_ffn_in['bg1'], 'L0_ffn_Wg2': _L0_ffn_in['Wg2'], 'L0_ffn_bg2': _L0_ffn_in['bg2'], 'L0_ffn_Wo': _L0_ffn_in['Wo'], 'L0_ffn_bo': _L0_ffn_in['bo'], 'L1_xattn_Wq': _L1_xattn_in['Wq'], 'L1_xattn_Wk': _L1_xattn_in['Wk'], 'L1_xattn_Wv': _L1_xattn_in['Wv'], 'L1_xattn_Wo': _L1_xattn_in['Wo'], 'L1_ffn_Wq': _L1_ffn_in['Wq'], 'L1_ffn_Wk': _L1_ffn_in['Wk'], 'L1_ffn_Wv': _L1_ffn_in['Wv'], 'L1_ffn_gate_W': _L1_ffn_in['gate_W'], 'L1_ffn_W1': _L1_ffn_in['W1'], 'L1_ffn_b1': _L1_ffn_in['b1'], 'L1_ffn_W2': _L1_ffn_in['W2'], 'L1_ffn_b2': _L1_ffn_in['b2'], 'L1_ffn_ln1_g': _L1_ffn_in['ln1_g'], 'L1_ffn_ln1_b': _L1_ffn_in['ln1_b'], 'L1_ffn_ln2_g': _L1_ffn_in['ln2_g'], 'L1_ffn_ln2_b': _L1_ffn_in['ln2_b']}

def reference(x, ctx_1024, L0_ffn_Wq, L0_ffn_bq, L0_ffn_Wk, L0_ffn_bk, L0_ffn_Wv, L0_ffn_bv, L0_ffn_Wg1, L0_ffn_bg1, L0_ffn_Wg2, L0_ffn_bg2, L0_ffn_Wo, L0_ffn_bo, L1_xattn_Wq, L1_xattn_Wk, L1_xattn_Wv, L1_xattn_Wo, L1_ffn_Wq, L1_ffn_Wk, L1_ffn_Wv, L1_ffn_gate_W, L1_ffn_W1, L1_ffn_b1, L1_ffn_W2, L1_ffn_b2, L1_ffn_ln1_g, L1_ffn_ln1_b, L1_ffn_ln2_g, L1_ffn_ln2_b):
    import jax
    import jax.numpy as jnp

    def _L0_xattn_ref(hidden_states, visual_hidden_state):
        import jax, jax.numpy as jnp
        import numpy as np
        scores = jnp.einsum('bld,bvd->blv', hidden_states, visual_hidden_state)
        probs = jax.nn.softmax(scores, axis=-1)
        return jnp.einsum('blv,bvd->bld', probs, visual_hidden_state)

    def _L0_ffn_ref(hidden_states, Wq, bq, Wk, bk, Wv, bv, Wg1, bg1, Wg2, bg2, Wo, bo):
        import jax, jax.numpy as jnp
        import numpy as np
        N_HEADS = 16
        NUM_EXPERTS = 4
        TOP_K = 2
        D_MODEL = 128
        GATE_HID = 128
        B, T, C = hidden_states.shape
        H = N_HEADS
        D = C // H
        pooled = hidden_states.mean(axis=1)
        logits = jax.nn.relu(pooled @ Wg1 + bg1) @ Wg2 + bg2
        vals, idx = jax.lax.top_k(logits, TOP_K)
        sm = jax.nn.softmax(vals, axis=-1)
        weights = jnp.zeros_like(logits).at[jnp.arange(B)[:, None], idx].set(sm)

        def moe_proj(W, b):
            Wc = jnp.einsum('be,ecd->bcd', weights, W)
            bc = weights @ b
            return jnp.einsum('btc,bcd->btd', hidden_states, Wc) + bc[:, None, :]
        q = moe_proj(Wq, bq).reshape(B, T, H, D)
        k = moe_proj(Wk, bk).reshape(B, T, H, D)
        v = moe_proj(Wv, bv).reshape(B, T, H, D)
        scores = jnp.einsum('bthd,bshd->bhts', q, k) / np.sqrt(D).astype(np.float32)
        attn = jax.nn.softmax(scores, axis=-1)
        out = jnp.einsum('bhts,bshd->bthd', attn, v).reshape(B, T, C)
        return out @ Wo + bo

    def _L1_xattn_ref(x_query, x_kv, Wq, Wk, Wv, Wo):
        import jax, jax.numpy as jnp
        import numpy as np
        DIM = 128
        NUM_HEADS = 16
        HEAD_DIM = DIM // NUM_HEADS
        ROPE_BASE = 10000.0
        SCALE = 1.0 / np.sqrt(HEAD_DIM)

        def _rotate_half(x):
            x1, x2 = jnp.split(x, 2, axis=-1)
            return jnp.concatenate([-x2, x1], axis=-1)

        def _rope(x, seq_len):
            inv_freq = 1.0 / ROPE_BASE ** (jnp.arange(0, HEAD_DIM, 2, dtype=jnp.float32) / HEAD_DIM)
            t = jnp.arange(seq_len, dtype=jnp.float32)
            freqs = jnp.outer(t, inv_freq)
            emb = jnp.concatenate([freqs, freqs], -1)
            cos = jnp.cos(emb)[None, None]
            sin = jnp.sin(emb)[None, None]
            return x * cos + _rotate_half(x) * sin
        B, T_q, _ = x_query.shape
        T_k = x_kv.shape[1]
        h, d = (NUM_HEADS, HEAD_DIM)
        q = (x_query @ Wq.T).reshape(B, T_q, h, d).transpose(0, 2, 1, 3)
        k = (x_kv @ Wk.T).reshape(B, T_k, h, d).transpose(0, 2, 1, 3)
        v = (x_kv @ Wv.T).reshape(B, T_k, h, d).transpose(0, 2, 1, 3)
        q = _rope(q, T_q)
        k = _rope(k, T_k)
        attn = jnp.einsum('bhqd,bhkd->bhqk', q, k) * SCALE
        attn = jax.nn.softmax(attn, axis=-1)
        out = jnp.einsum('bhqk,bhkd->bhqd', attn, v)
        out = out.transpose(0, 2, 1, 3).reshape(B, T_q, DIM)
        return out @ Wo.T

    def _L1_ffn_ref(x, Wq, Wk, Wv, gate_W, W1, b1, W2, b2, ln1_g, ln1_b, ln2_g, ln2_b):
        import jax, jax.numpy as jnp
        import numpy as np
        B, T, D, H, E, K = (2, 128, 128, 16, 8, 2)
        HS = D // H
        FF = 4 * D

        def layernorm(x, g, b, eps=1e-05):
            m = jnp.mean(x, axis=-1, keepdims=True)
            v = jnp.mean((x - m) ** 2, axis=-1, keepdims=True)
            return (x - m) * jax.lax.rsqrt(v + eps) * g + b
        b, t, d = x.shape
        q = jnp.einsum('btd,hdf->bhtf', x, Wq)
        k = jnp.einsum('btd,hdf->bhtf', x, Wk)
        v = jnp.einsum('btd,hdf->bhtf', x, Wv)
        wei = jnp.einsum('bhtf,bhsf->bhts', q, k) * d ** (-0.5)
        mask = jnp.tril(jnp.ones((t, t), bool))
        wei = jnp.where(mask, wei, -jnp.inf)
        wei = jax.nn.softmax(wei, axis=-1)
        attn = jnp.einsum('bhts,bhsf->bhtf', wei, v)
        attn = attn.transpose(0, 2, 1, 3).reshape(b, t, d)
        y = x + layernorm(attn, ln1_g, ln1_b)
        flat = y.reshape(-1, d)
        logits = flat @ gate_W
        topv, topi = jax.lax.top_k(logits, K)
        w = jax.nn.softmax(topv, axis=-1)
        combine = jnp.sum(jax.nn.one_hot(topi, E, dtype=flat.dtype) * w[..., None], axis=1)
        h = jax.nn.relu(jnp.einsum('nd,edf->enf', flat, W1) + b1[:, None, :])
        eo = jnp.einsum('enf,efd->end', h, W2) + b2[:, None, :]
        moe = jnp.einsum('ne,end->nd', combine, eo)
        out = y + layernorm(moe.reshape(b, t, d), ln2_g, ln2_b)
        return out
    x = x + _L0_xattn_ref(_layernorm(x, axis=-1), ctx_1024)
    x = x + _L0_ffn_ref(_layernorm(x, axis=-1), L0_ffn_Wq, L0_ffn_bq, L0_ffn_Wk, L0_ffn_bk, L0_ffn_Wv, L0_ffn_bv, L0_ffn_Wg1, L0_ffn_bg1, L0_ffn_Wg2, L0_ffn_bg2, L0_ffn_Wo, L0_ffn_bo)
    x = x + _L1_xattn_ref(_layernorm(x, axis=-1), ctx_1024, L1_xattn_Wq, L1_xattn_Wk, L1_xattn_Wv, L1_xattn_Wo)
    x = x + _L1_ffn_ref(_layernorm(x, axis=-1), L1_ffn_Wq, L1_ffn_Wk, L1_ffn_Wv, L1_ffn_gate_W, L1_ffn_W1, L1_ffn_b1, L1_ffn_W2, L1_ffn_b2, L1_ffn_ln1_g, L1_ffn_ln1_b, L1_ffn_ln2_g, L1_ffn_ln2_b)
    return x

_drawn_inputs = setup_inputs


def setup_inputs(seed=0):
    import zlib

    import numpy as np

    out = dict(_drawn_inputs(seed))
    spreads = {'L0_ffn_bq': (0.0, 0.332),
     'L0_ffn_bk': (0.0, 0.8),
     'L0_ffn_bv': (0.0, 0.1),
     'L0_ffn_bg1': (0.0, 0.1),
     'L0_ffn_bg2': (0.0, 0.1),
     'L0_ffn_bo': (0.0, 0.1),
     'L1_ffn_b1': (0.0, 0.1),
     'L1_ffn_b2': (0.0, 0.1),
     'L1_ffn_ln1_g': (1.0, 0.2),
     'L1_ffn_ln1_b': (0.0, 0.1),
     'L1_ffn_ln2_g': (1.0, 0.2),
     'L1_ffn_ln2_b': (0.0, 0.1)}
    factors = {'L1_ffn_Wq': 3.559, 'L1_ffn_Wk': 3.372}
    for name, (base, spread) in spreads.items():
        noise = np.random.default_rng([zlib.crc32(name.encode()), seed]).standard_normal(out[name].shape)
        drawn = base * np.exp(spread * noise) if base else spread * noise
        out[name] = jnp.asarray(drawn.astype(out[name].dtype))
    for name, factor in factors.items():
        out[name] = (out[name] * factor).astype(out[name].dtype)
    return out
```

```python
from contextlib import ExitStack

import numpy as np

import concourse.bass as bass
from concourse import mybir

F32 = mybir.dt.float32
F16 = mybir.dt.float16
ALU = mybir.AluOpType
ACT = mybir.ActivationFunctionType
X_AXIS = mybir.AxisListType.X

B, T, D, NKC = 16, 128, 128, 77
NH, HD = 16, 8
E0, E1, FF = 4, 8, 512
GROUP = 4
NS = 2
SPS = GROUP // NS
W = SPS * T
NG = B // GROUP
CH = FF // 128
UNITS = E1 * CH
NQ = 4
NT = NH // NQ
VW = HD + 1
EPS = 1e-5
LAYERS = ("B", "C", "D")
KEYS = {"B": T, "C": NKC, "D": T}
SCALE = {"B": HD ** -0.5, "C": HD ** -0.5, "D": D ** -0.5}
MASKED = -60000.0

PACK = (("ident", 128), ("w0", E0 * 3 * D), ("wg1", D), ("wo0", D), ("wq", D), ("wqp", D), ("wk", D), ("wkp", D),
        ("wv", D), ("wo1", D), ("dq", D), ("dk", D), ("dv", D), ("wg2", E0), ("gate", E1), ("bg1", 1),
        ("b0", 3 * E0), ("b1", UNITS), ("cos", T), ("sin", T), ("triL0", SPS * E0 * E0), ("triU0", SPS * E0 * E0),
        ("triL1", SPS * E1 * E1), ("triU1", SPS * E1 * E1))
PACK_AT, PACK_W = {}, 0
for _n, _w in PACK:
    PACK_AT[_n] = (PACK_W, PACK_W + _w)
    PACK_W += _w
ROWS = (("g1", D), ("b1", D), ("g2", D), ("b2", D), ("bg2", E0))
ROWS_AT, ROWS_W = {}, 0
for _n, _w in ROWS:
    ROWS_AT[_n] = (ROWS_W, ROWS_W + _w)
    ROWS_W += _w

HALF = (("ident16", 128), ("maskS", NT * T), ("maskST", NT * T), ("ones", NT * W), ("zeros", NT * W))
HALF_AT, HALF_W = {}, 0
for _n, _w in HALF:
    HALF_AT[_n] = (HALF_W, HALF_W + _w)
    HALF_W += _w

HOPS = ("ctxT", "A.xT", "A.s", "A.pT", "A.o", "C.k", "C.v",
        "B.xT", "B.hid", "B.lg", "B.qk", "B.v", "B.mt", "B.pv", "B.oT", "B.wo",
        "C.xT", "C.q", "C.mt", "C.pv", "C.oT", "C.wo",
        "D.xT", "D.qk", "D.v", "D.mt", "D.pv", "D.yT", "D.lg", "D.cT")
NORMS = ("A", "B", "C", "D", "D2")
STACK_DMAS = 3 * NT + 1
MAX_DMAS = NT


def schedule():
    FILL = [("fill",)]

    def moe(n):
        return [("moe",)] * n

    def head(s, L):
        if L == "B":
            return ([("hop", s, "B.xT")] + moe(1) + [("hop", s, "B.hid"), ("hop", s, "B.lg")] + moe(2)
                    + [("hop", s, "B.qk"), ("stack", s, "B"), ("hop", s, "B.v")])
        if L == "C":
            return [("hop", s, "C.xT")] + moe(1) + [("hop", s, "C.q"), ("stack", s, "C")]
        return [("hop", s, "D.xT")] + moe(1) + [("hop", s, "D.qk"), ("stack", s, "D"), ("hop", s, "D.v")]

    def tail(s, L):
        if L == "D":
            return [("hop", s, "D.pv"), ("ln1", s, "D2"), ("ln2", s, "D2"), ("y", s), ("hop", s, "D.yT"),
                    ("hop", s, "D.lg"), ("hop", s, "D.cT")]
        return [("hop", s, L + ".pv"), ("hop", s, L + ".oT")] + moe(1) + [("hop", s, L + ".wo")]

    def both(m, e):
        out = []
        for u in range(SPS * NQ):
            if m:
                out.append(("M", m[0], m[1], u))
            if e:
                out.append(("E", e[0], e[1], u))
        if m:
            out.append(("hop", m[0], m[1] + ".mt"))
        return out

    steps = [("moe_start",)]
    for s in range(NS):
        steps += [("load", s), ("hop", s, "ctxT"), ("ln1", s, "A")]
    steps += [("ln2", s, "A") for s in range(NS)]
    for h in ("A.xT", "A.s", "A.pT", "A.o"):
        steps += moe(1) + [("hop", s, h) for s in range(NS)]
    steps += [("ln1", s, "B") for s in range(NS)]
    steps += [("hop", s, h) for h in ("C.k", "C.v") for s in range(NS)]
    steps += [("ln2", s, "B") for s in range(NS)]
    steps += head(0, "B") + head(1, "B") + moe(1)
    steps += both((0, "B"), None)
    steps += both((1, "B"), (0, "B"))
    for L, N in (("B", "C"), ("C", "D")):
        for s in range(NS):
            steps += tail(s, L) + [("ln1", s, N)] + moe(1) + [("ln2", s, N)] + head(s, N)
            steps += FILL
            steps += both((s, N), (1 - s, L if s == 0 else N))
    steps += [("moe_end",)]
    steps += tail(0, "D")
    steps += both(None, (1, "D"))
    steps += tail(1, "D")
    left = UNITS - steps.count(("moe",))
    places = steps.count(FILL[0])
    for n in range(places):
        at = steps.index(FILL[0])
        steps[at:at + 1] = moe(left * (n + 1) // places - left * n // places)
    return steps


STEPS = schedule()


def numbered(kind):
    turns = {}
    for step in STEPS:
        if step[0] == kind and step[1:3] not in turns:
            turns[step[1:3]] = len(turns)
    return turns


M_TURN, E_TURN = numbered("M"), numbered("E")
N_CONST = 7
ATT_LINKS = 100
MOE_LINKS = 2
PASSES = len(M_TURN)
UPP = SPS * NQ


def build(nc, x, ctx, pack, rows, half, w1, w2, b2, bo, out):
    with ExitStack() as stack:
        def sb(name, shape, dt=F32):
            return stack.enter_context(nc.sbuf_tensor(name, shape, dt))

        def sem(name):
            return stack.enter_context(nc.semaphore(name))

        def per_stream(make, name, *a):
            return [make(f"{name}{s}", *a) for s in range(NS)]

        pk = sb("pk", [128, PACK_W])
        rw = sb("rw", [128, ROWS_W])
        hf = sb("hf", [128, HALF_W], F16)
        w1f = sb("w1f", [128, UNITS * 128])
        w1hi = sb("w1hi", [128, UNITS * 128], F16)
        w1lo = sb("w1lo", [128, UNITS * 128], F16)
        w2f = sb("w2f", [128, UNITS, D])
        b2f = sb("b2f", [E1, D])
        bof = sb("bof", [1, D])
        onesrow = sb("onesrow", [1, T])
        neghalf = sb("neghalf", [128, GROUP])

        def P(name, rows_=128):
            a, b = PACK_AT[name]
            return pk[0:rows_, a:b]

        def R(name):
            a, b = ROWS_AT[name]
            return rw[:, a:b]

        def H(name):
            a, b = HALF_AT[name]
            return hf[:, a:b]

        xin = per_stream(sb, "xin", [128, SPS, D])
        cin = per_stream(sb, "cin", [NKC, SPS, D])
        ctxT = per_stream(sb, "ctxT", [128, SPS * NKC])
        xs = per_stream(sb, "xs", [128, SPS, D])
        stats = per_stream(sb, "stats", [128, SPS, 6])
        mv = per_stream(sb, "mv", [128, SPS, 2])
        ve = per_stream(sb, "ve", [128, SPS])
        rstd = per_stream(sb, "rstd", [128, SPS])
        xn = per_stream(sb, "xn", [128, SPS, D])
        xnT = per_stream(sb, "xnT", [128, W])
        nmA = per_stream(sb, "nmA", [128, SPS])
        sumA = per_stream(sb, "sumA", [128, SPS])
        rinvA = per_stream(sb, "rinvA", [128, SPS])
        pA = per_stream(sb, "pA", [128, SPS, NKC])
        pAT = per_stream(sb, "pAT", [NKC, W])
        pooled = per_stream(sb, "pooled", [128, SPS])
        hid = per_stream(sb, "hid", [128, SPS])
        hidw = per_stream(sb, "hidw", [128, SPS, 128])
        lg = per_stream(sb, "lg", [128, SPS * E1])
        lmax = per_stream(sb, "lmax", [128, SPS])
        lsub = per_stream(sb, "lsub", [128, SPS * E1])
        lexp = per_stream(sb, "lexp", [128, SPS * E1])
        pair = per_stream(sb, "pair", [128, SPS * E1 * E1])
        above = per_stream(sb, "above", [128, SPS * E1 * E1])
        tied = per_stream(sb, "tied", [128, SPS * E1 * E1])
        rank = per_stream(sb, "rank", [128, SPS * E1])
        picked = per_stream(sb, "picked", [128, SPS * E1])
        psumw = per_stream(sb, "psumw", [128, SPS])
        gw = per_stream(sb, "gw", [128, SPS, E0])
        wc = per_stream(sb, "wc", [128, SPS, 3 * D])
        bmix = per_stream(sb, "bmix", [128, 3, SPS, E0])
        bqkv = per_stream(sb, "bqkv", [128, 3 * SPS])
        qkf = per_stream(sb, "qkf", [128, 2, W])
        rope1 = per_stream(sb, "rope1", [128, W])
        rope2 = per_stream(sb, "rope2", [128, W])
        hl = per_stream(sb, "hl", [128, 4, W], F16)
        hlC = per_stream(sb, "hlC", [128, 4, W], F16)
        qk = per_stream(sb, "qk", [128, 2, NT, W], F16)
        v9 = per_stream(sb, "v9", [128, SPS, NH, VW])
        v9C = per_stream(sb, "v9C", [NKC, SPS, NH, VW])
        negmax = per_stream(sb, "negmax", [128, SPS, NH])
        m8 = per_stream(sb, "m8", [128, SPS, NH, 8], F16)
        mT = per_stream(sb, "mT", [128, W], F16)
        rden = per_stream(sb, "rden", [128, SPS * NH])
        on = per_stream(sb, "on", [128, SPS, D])
        oT = per_stream(sb, "oT", [128, W])
        xnD = per_stream(sb, "xnD", [128, SPS, D])
        xnb = per_stream(sb, "xnb", [128, SPS, D])
        z = per_stream(sb, "z", [128, SPS, D])
        zg = per_stream(sb, "zg", [128, SPS, D])
        y = per_stream(sb, "y", [128, SPS, D])
        xy = per_stream(sb, "xy", [128, SPS, D])
        base = per_stream(sb, "base", [128, SPS, D])
        yT = per_stream(sb, "yT", [128, W])
        combT = per_stream(sb, "combT", [E1, W])
        probs = sb("probs", [128, 4, NT * T])
        yhi = sb("yhi", [128, GROUP * T], F16)
        ylo = sb("ylo", [128, GROUP * T], F16)
        comb = sb("comb", [128, GROUP, E1])
        hT = sb("hT", [128, 2, GROUP * T])
        acc = sb("acc", [128, GROUP, D])
        statsF = sb("statsF", [128, GROUP, 6])
        mvF = sb("mvF", [128, GROUP, 2])
        veF = sb("veF", [128, GROUP])
        rstdF = sb("rstdF", [128, GROUP])
        zF = sb("zF", [128, GROUP, D])
        zgF = sb("zgF", [128, GROUP, D])
        outb = sb("outb", [128, GROUP, D])

        scb = [stack.enter_context(nc.psum_tensor(f"scb{i}", [128, NT * T], F32)) for i in range(2)]
        stb = [stack.enter_context(nc.psum_tensor(f"stb{i}", [128, NT * T], F32)) for i in range(2)]
        mb = [stack.enter_context(nc.psum_tensor(f"mb{i}", [128, 512], F32)) for i in range(NS)]
        ub = stack.enter_context(nc.psum_tensor("ub", [128, GROUP * T], F32))
        db = stack.enter_context(nc.psum_tensor("db", [128, GROUP * D], F32))

        s_const = sem("s_const")
        s_w1hi, s_w1lo = sem("s_w1hi"), sem("s_w1lo")
        s_init_dve, s_init_pool = sem("s_init_dve"), sem("s_init_pool")
        s_ones = sem("s_ones")
        s_loaded = per_stream(sem, "s_loaded")
        s_hop = per_stream(sem, "s_hop")
        s_read = per_stream(sem, "s_read")
        s_ve = per_stream(sem, "s_ve")
        s_rstd = per_stream(sem, "s_rstd")
        s_xn = per_stream(sem, "s_xn")
        s_nmA = per_stream(sem, "s_nmA")
        s_hidw = per_stream(sem, "s_hidw")
        s_lsub = per_stream(sem, "s_lsub")
        s_lexp = per_stream(sem, "s_lexp")
        s_wc = per_stream(sem, "s_wc")
        s_qkf = per_stream(sem, "s_qkf")
        s_hi = per_stream(sem, "s_hi")
        s_hl = per_stream(sem, "s_hl")
        s_stack = per_stream(sem, "s_stack")
        s_m8 = per_stream(sem, "s_m8")
        s_max = per_stream(sem, "s_max")
        s_on = per_stream(sem, "s_on")
        s_xnb = per_stream(sem, "s_xnb")
        s_y = per_stream(sem, "s_y")
        s_base = per_stream(sem, "s_base")
        s_comb = per_stream(sem, "s_comb")
        s_sc, s_scread = sem("s_sc"), sem("s_scread")
        s_st, s_exp, s_pv = sem("s_st"), sem("s_exp"), sem("s_pv")
        s_y16 = sem("s_y16")
        s_up, s_relu, s_down = sem("s_up"), sem("s_relu"), sem("s_down")
        s_accinit, s_acc = sem("s_accinit"), sem("s_acc")
        s_veF, s_rstdF, s_zF = sem("s_veF"), sem("s_rstdF"), sem("s_zF")
        s_outb, s_store = sem("s_outb"), sem("s_store")
        s_passed = per_stream(sem, "s_passed")
        c_dve = sem("c_dve")
        c_moe = sem("c_moe")
        c_pool, c_poolF = sem("c_pool"), sem("c_poolF")

        def after(eng, s, value):
            if not (isinstance(value, int) and value <= 0):
                eng.wait_ge(s, value)

        def hop(g, name):
            return g * len(HOPS) + HOPS.index(name) + 1

        def read(g, name):
            return hop(g, name) + 1

        def layer(g, L, per=1):
            return (g * len(LAYERS) + LAYERS.index(L)) * per

        def norm(g, N):
            return g * len(NORMS) + NORMS.index(N) + 1

        def m_unit(g, s, L, u):
            return (g * PASSES + M_TURN[s, L]) * UPP + u

        def e_unit(g, s, L, u):
            return (g * PASSES + E_TURN[s, L]) * UPP + u

        def values(s, L):
            return v9C[s] if L == "C" else v9[s]

        def run(eng, step):
            for st in STEPS:
                step(0, None, st)
            with eng.Fori(1, NG) as g:
                for st in STEPS:
                    step(g, g - 1, st)
            for st in STEPS:
                step(None, NG - 1, st)

        block = stack.enter_context(nc.Block())

        @block.sync
        def _(sp):
            for dst, src in ((pk, pack), (hf, half), (w1f, w1), (w2f, w2), (b2f, b2), (bof, bo)):
                sp.dma_start(dst[:], src).then_inc(s_const, 16)
            sp.dma_start(rw[:], rows.partition_broadcast(128)).then_inc(s_const, 16)
            sp.wait_ge(s_const, N_CONST * 16)
            for s in range(NS):
                sp.dma_start(qk[s][3:128:4, 1, :, :], H("ones")[0:32].rearrange("p (t w) -> p t w", t=NT)
                             ).then_inc(s_ones, 16)

            def step(g, gm, st):
                kind = st[0]
                if kind == "load" and g is not None:
                    s = st[1]
                    after(sp, s_read[s], read(g - 1, "A.o") if not isinstance(g, int) or g else 0)
                    sp.sem_inc(s_passed[1], 1)
                    b0 = g * GROUP + s * SPS
                    sp.dma_start(xin[s][:], x[bass.ds(b0, SPS)].rearrange("b t d -> t b d")
                                 ).then_inc(s_loaded[s], 16)
                    sp.dma_start(cin[s][:], ctx[bass.ds(b0, SPS)].rearrange("b t d -> t b d")
                                 ).then_inc(s_loaded[s], 16)
                elif kind == "stack" and g is not None:
                    _, s, L = st
                    if L != "B":
                        sp.wait_ge(s_st, e_unit(g, s, LAYERS[LAYERS.index(L) - 1], UPP - 1) + 1)
                    elif not isinstance(g, int):
                        sp.wait_ge(s_st, e_unit(g - 1, s, "D", UPP - 1) + 1)
                    sp.sem_inc(s_passed[1], 1)
                    sp.wait_ge(s_hl[s], layer(g, L) + 1)
                    src = hlC[s] if L == "C" else hl[s]
                    for t in range(NT):
                        rows_ = slice(32 * t, 32 * t + 32)
                        for r, pick in enumerate((src[rows_, 0:4:2, :], src[rows_, 0:4:3, :], src[rows_, 1:3, :])):
                            sp.dma_start(qk[s][r:128:4, :, t, :], pick).then_inc(s_stack[s], 16)
                    sp.dma_start(qk[s][3:128:4, 0, :, :], H("zeros")[0:32].rearrange("p (t w) -> p t w", t=NT)
                                 ).then_inc(s_stack[s], 16)
                elif kind == "hop" and g is not None and st[2].endswith("mt"):
                    _, s, h = st
                    sp.wait_ge(s_read[s], read(g, h))
                    for t in range(NT):
                        sp.dma_start(qk[s][3:128:4, 0, t, :], mT[s][32 * t:32 * t + 32, :]
                                     ).then_inc(s_max[s], 16)
                elif kind == "moe_end" and gm is not None:
                    sp.wait_ge(s_outb, gm + 1)
                    sp.sem_inc(s_passed[1], 1)
                    sp.dma_start(out[bass.ds(gm * GROUP, GROUP)].rearrange("b t d -> t b d"), outb[:]
                                 ).then_inc(s_store, 16)

            run(sp, step)
            sp.wait_ge(s_store, 1 + 16 * NG)

        @block.tensor
        def _(pe):
            mm = pe.matmul
            ident, ident16 = P("ident"), H("ident16")

            def hop_step(g, s, h):
                bank = mb[s]
                pe.wait_ge(s_read[s], hop(g, h))
                if h == "ctxT":
                    pe.wait_ge(s_loaded[s], 32 * (g + 1))
                    for i in range(SPS):
                        last = pe.transpose(bank[:, i * NKC:(i + 1) * NKC], cin[s][:, i, :], P("ident", NKC)[:, 0:NKC])
                elif h in ("A.xT", "B.xT", "C.xT", "D.xT"):
                    N = h[0]
                    pe.wait_ge(s_xn[s], norm(g, N))
                    src = xnD[s] if N == "D" else xn[s]
                    for i in range(SPS):
                        last = pe.transpose(bank[:, i * T:(i + 1) * T], src[:, i, :], ident)
                elif h == "A.s":
                    for i in range(SPS):
                        last = mm(bank[:, i * NKC:(i + 1) * NKC], xnT[s][:, i * T:(i + 1) * T],
                                  ctxT[s][:, i * NKC:(i + 1) * NKC], start=True, stop=True)
                elif h == "A.pT":
                    for i in range(SPS):
                        last = pe.transpose(bank[0:NKC, i * T:(i + 1) * T], pA[s][:, i, :], ident)
                elif h == "A.o":
                    for i in range(SPS):
                        last = mm(bank[:, i * D:(i + 1) * D], pAT[s][:, i * T:(i + 1) * T], cin[s][:, i, :],
                                  start=True, stop=True)
                elif h == "C.k":
                    mm(bank[:, 0:SPS * NKC], P("wk"), ctxT[s][:], start=True, stop=True)
                    last = mm(bank[:, 256:256 + SPS * NKC], P("wkp"), ctxT[s][:], start=True, stop=True)
                elif h == "C.v":
                    for i in range(SPS):
                        last = mm(bank[0:NKC, i * D:(i + 1) * D], ctxT[s][:, i * NKC:(i + 1) * NKC], P("wv"),
                                  start=True, stop=True)
                elif h == "B.hid":
                    last = mm(bank[:, 0:SPS], P("wg1"), pooled[s][:], start=True, stop=True)
                elif h == "B.lg":
                    pe.wait_ge(s_hidw[s], g + 1)
                    for i in range(SPS):
                        last = mm(bank[:, i * E0:(i + 1) * E0], hidw[s][:, i, :], P("wg2"), start=True, stop=True)
                elif h == "B.qk":
                    pe.wait_ge(s_wc[s], g + 1)
                    for n in range(2):
                        for i in range(SPS):
                            last = mm(bank[:, n * W + i * T:n * W + (i + 1) * T], wc[s][:, i, n * D:(n + 1) * D],
                                      xnT[s][:, i * T:(i + 1) * T], start=True, stop=True)
                elif h == "B.v":
                    for i in range(SPS):
                        last = mm(bank[:, i * D:(i + 1) * D], xnT[s][:, i * T:(i + 1) * T],
                                  wc[s][:, i, 2 * D:3 * D], start=True, stop=True)
                elif h in ("C.q", "D.qk"):
                    a, b = ("wq", "wqp") if h == "C.q" else ("dq", "dk")
                    mm(bank[:, 0:W], P(a), xnT[s][:], start=True, stop=True)
                    last = mm(bank[:, W:2 * W], P(b), xnT[s][:], start=True, stop=True)
                elif h == "D.v":
                    for i in range(SPS):
                        last = mm(bank[:, i * D:(i + 1) * D], xnT[s][:, i * T:(i + 1) * T], P("dv"),
                                  start=True, stop=True)
                elif h.endswith("mt"):
                    pe.wait_ge(s_m8[s], layer(g, h[0], SPS) + SPS)
                    half_bank = bank[:].bitcast(F16)
                    for i in range(SPS):
                        last = pe.transpose(half_bank[:, i * T:(i + 1) * T],
                                            m8[s][:, i, :, :].rearrange("p h e -> p (h e)"), ident16)
                elif h.endswith("oT"):
                    pe.wait_ge(s_on[s], layer(g, h[0]) + 1)
                    for i in range(SPS):
                        last = pe.transpose(bank[:, i * T:(i + 1) * T], on[s][:, i, :], ident)
                elif h.endswith("wo"):
                    for i in range(SPS):
                        last = mm(bank[:, i * D:(i + 1) * D], oT[s][:, i * T:(i + 1) * T],
                                  P("wo0" if h[0] == "B" else "wo1"), start=True, stop=h[0] == "C")
                        if h[0] == "B":
                            last = mm(bank[:, i * D:(i + 1) * D], onesrow[:], bof[:], start=False, stop=True)
                elif h == "D.yT":
                    pe.wait_ge(s_y[s], g + 1)
                    for i in range(SPS):
                        last = pe.transpose(bank[:, i * T:(i + 1) * T], y[s][:, i, :], ident)
                elif h == "D.lg":
                    for i in range(SPS):
                        last = mm(bank[:, i * E1:(i + 1) * E1], yT[s][:, i * T:(i + 1) * T], P("gate"),
                                  start=True, stop=True)
                elif h == "D.cT":
                    pe.wait_ge(s_comb[s], g + 1)
                    for i in range(SPS):
                        last = pe.transpose(bank[0:E1, i * T:(i + 1) * T], comb[:, s * SPS + i, :], ident)
                last.then_inc(s_hop[s], 1)

            def stack_rows(s, n, q, t, i, width):
                return qk[s][32 * q:32 * q + 32, n, t, i * T:i * T + width]

            def weighted(g, s, L, u):
                i, q = divmod(u, NQ)
                n = e_unit(g, s, L, u)
                if u == 0:
                    pe.wait_ge(s_read[s], hop(g, L + ".pv"))
                    pe.wait_ge(s_read[s], read(g, L + ".v"))
                pe.wait_ge(s_exp, n + 3)
                nk = KEYS[L]
                for t in range(NT):
                    h = NQ * t + q
                    last = mm(mb[s][:, (i * NH + h) * VW:(i * NH + h + 1) * VW],
                              probs[0:nk, u % 4, t * T:(t + 1) * T], values(s, L)[0:nk, i, h, :],
                              start=True, stop=True)
                last.then_inc(s_pv, 1)

            def down(gm, k):
                e, c = divmod(k, CH)
                if c == 0:
                    pe.wait_ge(s_acc, gm * (E1 + 1) + e + 2)
                pe.wait_ge(s_relu, gm * UNITS + k + 2)
                for i in range(GROUP):
                    last = mm(db[:, i * D:(i + 1) * D], hT[:, k % 2, i * T:(i + 1) * T], w2f[:, k, :],
                              start=c == 0 and i == 0, stop=c == CH - 1, skip_group_check=True)
                last.then_inc(s_down, 1)

            moe_at = [0]

            def step(g, gm, st):
                kind = st[0]
                if kind == "hop" and g is not None and not st[2].endswith("pv"):
                    hop_step(g, st[1], st[2])
                elif kind == "M" and g is not None:
                    _, s, L, u = st
                    i, q = divmod(u, NQ)
                    n, nk = m_unit(g, s, L, u), KEYS[L]
                    if u == 0:
                        pe.wait_ge(s_stack[s], (layer(g, L) + 1) * 16 * STACK_DMAS)
                    pe.wait_ge(s_scread, n + 1)
                    bank = scb[u % 2]
                    for t in range(NT):
                        last = mm(bank[:, t * nk:(t + 1) * nk], stack_rows(s, 0, q, t, i, T),
                                  stack_rows(s, 1, q, t, i, nk), start=L != "D" or t == 0, stop=L != "D")
                    if L == "D":
                        last = mm(bank[:], ident16, H("maskS"), start=False, stop=True)
                    last.then_inc(s_sc, 1)
                elif kind == "E" and g is not None:
                    _, s, L, u = st
                    i, q = divmod(u, NQ)
                    n, nk = e_unit(g, s, L, u), KEYS[L]
                    if u == 0:
                        pe.wait_ge(s_max[s], (layer(g, L) + 1) * 16 * MAX_DMAS)
                    pe.wait_ge(s_exp, n + 1)
                    bank = stb[u % 2]
                    for t in range(NT):
                        last = mm(bank[0:nk, t * T:(t + 1) * T], stack_rows(s, 1, q, t, i, nk),
                                  stack_rows(s, 0, q, t, i, T), start=L != "D" or t == 0, stop=L != "D")
                    if L == "D":
                        last = mm(bank[:], ident16, H("maskST"), start=False, stop=True)
                    last.then_inc(s_st, 1)
                    if u:
                        weighted(g, s, L, u - 1)
                    if u == UPP - 1:
                        weighted(g, s, L, u)
                elif kind == "moe_start" and gm is not None:
                    moe_at[0] = 0
                    pe.wait_ge(s_acc, gm * (E1 + 1) + 1)
                    for i in range(GROUP):
                        s = i // SPS
                        if i % SPS == 0:
                            pe.wait_ge(s_read[s], read(gm, "D.cT"))
                        last = mm(db[:, i * D:(i + 1) * D], combT[s][:, (i % SPS) * T:(i % SPS + 1) * T], b2f[:],
                                  start=True, stop=True)
                    last.then_inc(s_accinit, 1)
                    pe.wait_ge(s_y16, NS * (gm + 1))
                elif kind == "moe" and gm is not None:
                    k = moe_at[0]
                    moe_at[0] += 1
                    pe.wait_ge(s_relu, gm * UNITS + k + 1)
                    a, b = k * 128, (k + 1) * 128
                    mm(ub[:], w1hi[:, a:b], yhi[:], start=True, stop=False)
                    mm(ub[:], w1hi[:, a:b], ylo[:], start=False, stop=False)
                    mm(ub[:], w1lo[:, a:b], yhi[:], start=False, stop=True).then_inc(s_up, 1)
                    if k:
                        down(gm, k - 1)
                elif kind == "moe_end" and gm is not None:
                    down(gm, UNITS - 1)

            pe.wait_ge(s_const, N_CONST * 16)
            pe.wait_ge(s_w1lo, 1)
            pe.wait_ge(s_w1hi, 1)
            pe.wait_ge(s_init_dve, 1)
            pe.wait_ge(s_init_pool, 1)
            pe.wait_ge(s_ones, 16 * NS)
            run(pe, step)

        @block.scalar
        def _(act):
            moe_at = [0]

            def hop_step(g, s, h):
                bank = mb[s]
                if h not in ("ctxT", "A.xT", "A.s", "A.pT", "C.v", "B.xT", "B.hid", "B.lg", "B.qk", "B.v", "B.mt",
                             "C.xT", "C.mt", "C.oT", "D.xT", "D.qk", "D.v", "D.mt", "D.yT", "D.lg"):
                    return
                if h in ("B.lg", "D.lg"):
                    n = SPS * (E0 if h == "B.lg" else E1)
                    act.wait_ge(s_lsub[s], 2 * g + (1 if h == "B.lg" else 2))
                    act.activation(lexp[s][:, 0:n], lsub[s][:, 0:n], ACT.Exp).then_inc(s_lexp[s], 1)
                    return
                if h == "B.qk":
                    act.wait_ge(s_qkf[s], g + 1)
                    act.activation(hl[s][:, 0:4:2, :], qkf[s][:], ACT.Copy).then_inc(s_hi[s], 1)
                    return
                act.wait_ge(s_hop[s], hop(g, h))
                if h == "A.s":
                    act.wait_ge(s_nmA[s], g + 1)
                    for i in range(SPS):
                        last = act.activation(pA[s][:, i, :], bank[:, i * NKC:(i + 1) * NKC], ACT.Exp,
                                              bias=nmA[s][:, i:i + 1], accum_out=sumA[s][:, i:i + 1])
                elif h == "ctxT":
                    last = act.activation(ctxT[s][:], bank[:, 0:SPS * NKC], ACT.Copy)
                elif h == "B.xT":
                    for i in range(SPS):
                        last = act.activation(xnT[s][:, i * T:(i + 1) * T], bank[:, i * T:(i + 1) * T], ACT.Copy,
                                              accum_out=pooled[s][:, i:i + 1])
                elif h in ("A.xT", "C.xT", "D.xT"):
                    last = act.activation(xnT[s][:], bank[:, 0:W], ACT.Copy)
                elif h == "A.pT":
                    last = act.activation(pAT[s][:], bank[0:NKC, 0:W], ACT.Copy)
                elif h == "B.hid":
                    last = act.activation(hid[s][:], bank[:, 0:SPS], ACT.Relu, bias=P("bg1"), scale=1.0 / T)
                elif h in ("B.v", "D.v", "C.v"):
                    dst = v9C[s] if h == "C.v" else v9[s]
                    nk = KEYS[h[0]]
                    last = act.activation(dst[:, :, :, 0:HD].rearrange("p i h e -> p (i h) e"),
                                          bank[0:nk, 0:W].rearrange("p (n e) -> p n e", e=HD), ACT.Copy)
                elif h.endswith("mt"):
                    last = act.activation(mT[s][:], bank[:].bitcast(F16)[:, 0:W], ACT.Copy)
                elif h == "C.oT":
                    last = act.activation(oT[s][:], bank[:, 0:W], ACT.Copy)
                elif h == "D.qk":
                    act.activation(hl[s][:, 0:4:2, :], bank[:].rearrange("p (n w) -> p n w", n=2), ACT.Copy
                                   ).then_inc(s_hi[s], 1)
                    return
                elif h == "D.yT":
                    last = act.activation(yT[s][:], bank[:, 0:W], ACT.Copy)
                last.then_inc(s_read[s], 1)

            def step(g, gm, st):
                kind = st[0]
                if kind == "hop" and g is not None:
                    hop_step(g, st[1], st[2])
                elif kind == "E" and g is not None:
                    _, s, L, u = st
                    n, nk = e_unit(g, s, L, u), KEYS[L]
                    act.wait_ge(s_st, n + 1)
                    act.wait_ge(s_pv, n + 1)
                    act.activation(probs[0:nk, u % 4, :], stb[u % 2][0:nk, :], ACT.Exp, scale=SCALE[L]
                                   ).then_inc(s_exp, 1)
                elif kind == "moe_start":
                    moe_at[0] = 0
                elif kind == "moe" and gm is not None:
                    k = moe_at[0]
                    moe_at[0] += 1
                    act.wait_ge(s_up, gm * UNITS + k + 1)
                    act.wait_ge(s_down, gm * UNITS + k + 1)
                    act.activation(hT[:, k % 2, :], ub[:], ACT.Relu, bias=P("b1")[:, k:k + 1]).then_inc(s_relu, 1)

            act.wait_ge(s_const, N_CONST * 16)
            act.wait_ge(s_init_dve, 1)
            run(act, step)

        @block.vector
        def _(dve):
            att = [0]
            moe = [0]
            moe_at = [0]

            def link(g, ins):
                att[0] += 1
                ins.then_inc(c_dve, 1)
                dve.wait_ge(c_dve, g * ATT_LINKS + att[0])

            def link_moe(gm, ins):
                moe[0] += 1
                ins.then_inc(c_moe, 1)
                dve.wait_ge(c_moe, gm * MOE_LINKS + moe[0])

            def top2(g, s, bank, E, dst, bias, triL, triU, turn):
                n = SPS * E

                def v3(t):
                    return t[:, 0:n].rearrange("p (i e) -> p i e", i=SPS)

                lg3, sub3, exp3 = v3(lg[s]), v3(lsub[s]), v3(lexp[s])
                pr4 = pair[s][:, 0:n * E].rearrange("p (i e f) -> p i e f", i=SPS, e=E)
                src = bank[:, 0:n].rearrange("p (i e) -> p i e", i=SPS)
                if bias is not None:
                    ins = dve.tensor_tensor(lg3, src, bias.unsqueeze(1).to_broadcast((128, SPS, E)), ALU.add)
                else:
                    ins = dve.tensor_copy(lg3, src)
                ins.then_inc(s_read[s], 1)
                dve.wait_ge(s_read[s], read(g, "B.lg" if E == E0 else "D.lg"))
                link(g, dve.tensor_reduce(lmax[s][:], lg3, X_AXIS, ALU.max))
                dve.tensor_tensor(sub3, lg3, lmax[s][:].unsqueeze(2).to_broadcast((128, SPS, E)),
                                  ALU.subtract).then_inc(s_lsub[s], 1)
                for i in range(SPS):
                    ins = dve.tensor_tensor(pr4[:, i], lg3[:, i].unsqueeze(1).to_broadcast((128, E, E)),
                                            lg3[:, i].unsqueeze(2).to_broadcast((128, E, E)), ALU.subtract)
                link(g, ins)
                dve.scalar_tensor_tensor(out=above[s][:, 0:n * E], in0=pair[s][:, 0:n * E], scalar=0.0, in1=triU,
                                         op0=ALU.is_gt, op1=ALU.mult)
                link(g, dve.scalar_tensor_tensor(out=tied[s][:, 0:n * E], in0=pair[s][:, 0:n * E], scalar=0.0,
                                                 in1=triL, op0=ALU.is_ge, op1=ALU.mult))
                link(g, dve.tensor_tensor(pair[s][:, 0:n * E], above[s][:, 0:n * E], tied[s][:, 0:n * E], ALU.add))
                link(g, dve.tensor_reduce(rank[s][:, 0:n], pair[s][:, 0:n * E].rearrange("p (n f) -> p n f", f=E),
                                          X_AXIS, ALU.add))
                dve.wait_ge(s_lexp[s], 2 * g + turn)
                link(g, dve.scalar_tensor_tensor(out=picked[s][:, 0:n], in0=rank[s][:, 0:n], scalar=2.0,
                                                 in1=lexp[s][:, 0:n], op0=ALU.is_lt, op1=ALU.mult))
                link(g, dve.tensor_reduce(psumw[s][:], v3(picked[s]), X_AXIS, ALU.add))
                link(g, dve.reciprocal(lmax[s][:], psumw[s][:]))
                return dve.tensor_tensor(dst, v3(picked[s]), lmax[s][:].unsqueeze(2).to_broadcast((128, SPS, E)),
                                         ALU.mult)

            def rope(g, s, h, n, hi, lo):
                bank = mb[s]
                dve.wait_ge(s_hop[s], hop(g, h))

                def v3(t):
                    return t[:, 0:SPS * n].rearrange("p (i w) -> p i w", i=SPS)

                cos = P("cos")[:, 0:n].unsqueeze(1).to_broadcast((128, SPS, n))
                sin = P("sin")[:, 0:n].unsqueeze(1).to_broadcast((128, SPS, n))
                dve.tensor_tensor(v3(rope1[s]), v3(bank), cos, ALU.mult)
                dve.tensor_tensor(v3(rope2[s]), bank[:, 256:256 + SPS * n].rearrange("p (i w) -> p i w", i=SPS), sin,
                                  ALU.mult).then_inc(s_read[s], 1)
                dve.wait_ge(s_read[s], read(g, h))
                link(g, dve.tensor_tensor(qkf[s][:, 0, 0:SPS * n], rope1[s][:, 0:SPS * n], rope2[s][:, 0:SPS * n],
                                          ALU.add))
                link(g, dve.tensor_copy(hi, v3(qkf[s][:, 0, :])))
                return dve.tensor_tensor(lo, v3(qkf[s][:, 0, :]), hi, ALU.subtract)

            def hop_step(g, s, h):
                bank = mb[s]
                halves = bank[:].rearrange("p (n w) -> p n w", n=2)
                if h == "A.s":
                    dve.wait_ge(s_hop[s], hop(g, h))
                    dve.tensor_reduce(nmA[s][:], bank[:, 0:SPS * NKC].rearrange("p (i k) -> p i k", i=SPS), X_AXIS,
                                      ALU.max, negate=True).then_inc(s_nmA[s], 1)
                elif h == "A.o":
                    dve.wait_ge(s_hop[s], hop(g, h))
                    link(g, dve.reciprocal(rinvA[s][:], sumA[s][:]))
                    after(dve, s_base[s], g)
                    for i in range(SPS):
                        last = dve.scalar_tensor_tensor(out=xs[s][:, i, :], in0=bank[:, i * D:(i + 1) * D],
                                                        scalar=rinvA[s][:, i:i + 1], in1=xin[s][:, i, :],
                                                        op0=ALU.mult, op1=ALU.add)
                    last.then_inc(s_read[s], 1)
                elif h == "C.k":
                    k4 = hlC[s][:, 2:4, :].rearrange("p n (i w) -> p n i w", i=SPS)
                    link(g, rope(g, s, h, NKC, k4[:, 0, :, 0:NKC], k4[:, 1, :, 0:NKC]))
                elif h == "C.q":
                    q4 = hlC[s][:, 0:2, :].rearrange("p n (i w) -> p n i w", i=SPS)
                    rope(g, s, h, T, q4[:, 0], q4[:, 1]).then_inc(s_hl[s], 1)
                elif h == "B.hid":
                    dve.wait_ge(s_read[s], read(g, h))
                    dve.tensor_copy(hidw[s][:], hid[s][:].unsqueeze(2).to_broadcast((128, SPS, 128))
                                    ).then_inc(s_hidw[s], 1)
                elif h == "B.lg":
                    dve.wait_ge(s_hop[s], hop(g, h))
                    link(g, top2(g, s, bank, E0, gw[s][:], R("bg2"), P("triL0"), P("triU0"), 1))
                    w0 = P("w0").rearrange("p (e w) -> p e w", e=E0)
                    for e in range(E0):
                        for i in range(SPS):
                            if e == 0:
                                ins = dve.tensor_scalar(wc[s][:, i, :], w0[:, e, :], gw[s][:, i, e:e + 1], None,
                                                        ALU.mult)
                            else:
                                ins = dve.scalar_tensor_tensor(out=wc[s][:, i, :], in0=w0[:, e, :],
                                                               scalar=gw[s][:, i, e:e + 1], in1=wc[s][:, i, :],
                                                               op0=ALU.mult, op1=ALU.add)
                        if e < E0 - 1:
                            link(g, ins)
                    ins.then_inc(s_wc[s], 1)
                    b0 = P("b0").rearrange("p (n e) -> p n e", n=3)
                    for n in range(3):
                        ins = dve.tensor_tensor(bmix[s][:, n], b0[:, n, :].unsqueeze(1).to_broadcast((128, SPS, E0)),
                                                gw[s][:], ALU.mult)
                    link(g, ins)
                    link(g, dve.tensor_reduce(bqkv[s][:], bmix[s][:].rearrange("p n i e -> p (n i) e"), X_AXIS,
                                              ALU.add))
                elif h == "B.qk":
                    dve.wait_ge(s_hop[s], hop(g, h))
                    dve.tensor_tensor(qkf[s][:].rearrange("p n (i w) -> p (n i) w", i=SPS),
                                      bank[:].rearrange("p (m w) -> p m w", w=T),
                                      bqkv[s][:, 0:2 * SPS].unsqueeze(2).to_broadcast((128, 2 * SPS, T)), ALU.add
                                      ).then_inc(s_qkf[s], 1)
                    dve.wait_ge(s_qkf[s], g + 1)
                    dve.sem_inc(s_read[s], 1)
                    dve.wait_ge(s_hi[s], 2 * g + 1)
                    dve.tensor_tensor(hl[s][:, 1:4:2, :], qkf[s][:], hl[s][:, 0:4:2, :], ALU.subtract
                                      ).then_inc(s_hl[s], 1)
                elif h == "D.qk":
                    dve.wait_ge(s_hi[s], 2 * g + 2)
                    link(g, dve.tensor_tensor(hl[s][:, 1:4:2, :], halves, hl[s][:, 0:4:2, :], ALU.subtract))
                    dve.sem_inc(s_hl[s], 1)
                    dve.sem_inc(s_read[s], 1)
                elif h.endswith("pv"):
                    n = e_unit(g, s, h[0], UPP - 1)
                    dve.wait_ge(s_pv, n + 5)
                    o3 = bank[:, 0:SPS * NH * VW].rearrange("p (n e) -> p n e", e=VW)
                    link(g, dve.reciprocal(rden[s][:].unsqueeze(2), o3[:, :, HD:VW]))
                    dve.tensor_tensor(on[s][:].rearrange("p i (h e) -> p (i h) e", e=HD), o3[:, :, 0:HD],
                                      rden[s][:].unsqueeze(2).to_broadcast((128, SPS * NH, HD)), ALU.mult
                                      ).then_inc(s_on[s], 1)
                    dve.wait_ge(s_on[s], layer(g, h[0]) + 1)
                    dve.sem_inc(s_hop[s], 1)
                    dve.sem_inc(s_read[s], 1)
                elif h == "B.oT":
                    dve.wait_ge(s_hop[s], hop(g, h))
                    for i in range(SPS):
                        last = dve.tensor_scalar(oT[s][:, i * T:(i + 1) * T], bank[:, i * T:(i + 1) * T],
                                                 bqkv[s][:, 2 * SPS + i:2 * SPS + i + 1], None, ALU.add)
                    last.then_inc(s_read[s], 1)
                elif h.endswith("wo"):
                    dve.wait_ge(s_hop[s], hop(g, h))
                    dve.tensor_tensor(xs[s][:].rearrange("p i d -> p (i d)"), bank[:, 0:W],
                                      xs[s][:].rearrange("p i d -> p (i d)"), ALU.add).then_inc(s_read[s], 1)
                elif h == "D.yT":
                    dve.wait_ge(s_read[s], read(g, h))
                    a, b = s * W, (s + 1) * W
                    link(g, dve.tensor_copy(yhi[:, a:b], yT[s][:]))
                    dve.tensor_tensor(ylo[:, a:b], yT[s][:], yhi[:, a:b], ALU.subtract).then_inc(s_y16, 1)
                elif h == "D.lg":
                    dve.wait_ge(s_hop[s], hop(g, h))
                    top2(g, s, bank, E1, comb[:, s * SPS:(s + 1) * SPS, :], None, P("triL1"), P("triU1"), 2
                         ).then_inc(s_comb[s], 1)
                elif h == "D.cT":
                    dve.wait_ge(s_hop[s], hop(g, h))
                    dve.tensor_copy(combT[s][:], bank[0:E1, 0:W]).then_inc(s_read[s], 1)

            def take_up(gm, e):
                dve.wait_ge(s_down, gm * UNITS + (e + 1) * CH + 2)
                for i in range(GROUP):
                    last = dve.scalar_tensor_tensor(out=acc[:, i, :], in0=db[:, i * D:(i + 1) * D],
                                                    scalar=comb[:, i, e:e + 1], in1=acc[:, i, :],
                                                    op0=ALU.mult, op1=ALU.add)
                last.then_inc(s_acc, 1)
                dve.wait_ge(s_acc, gm * (E1 + 1) + e + 3)

            def step(g, gm, st):
                kind = st[0]
                if kind == "ln1" and g is not None:
                    _, s, N = st
                    if N == "A":
                        dve.wait_ge(s_loaded[s], 32 * (g + 1))
                    elif N == "B":
                        dve.wait_ge(s_read[s], read(g, "A.o"))
                    elif N == "D2":
                        dve.wait_ge(s_on[s], layer(g, "D") + 1)
                    else:
                        dve.wait_ge(s_read[s], read(g, {"C": "B.wo", "D": "C.wo"}[N]))
                    src = {"A": xin, "D2": on}.get(N, xs)[s]
                    for i in range(SPS):
                        ins = dve.bn_stats(stats[s][:, i, :], src[:, i, :])
                    link(g, ins)
                    dve.sem_inc(s_passed[0], 1)
                    for i in range(SPS):
                        ins = dve.bn_aggr(mv[s][:, i, :], stats[s][:, i, :])
                    link(g, ins)
                    dve.tensor_scalar(ve[s][:], mv[s][:, :, 1], EPS, None, ALU.add).then_inc(s_ve[s], 1)
                elif kind == "ln2" and g is not None:
                    _, s, N = st
                    dve.wait_ge(s_rstd[s], norm(g, N))
                    src = {"A": xin, "D2": on}.get(N, xs)[s]
                    dst = {"D": xnD, "D2": z}.get(N, xn)[s]
                    for i in range(SPS):
                        last = dve.tensor_scalar(dst[:, i, :], src[:, i, :], mv[s][:, i, 0:1], rstd[s][:, i:i + 1],
                                                 ALU.subtract, ALU.mult)
                    last.then_inc(s_xn[s], 1)
                elif kind == "y" and g is not None:
                    s = st[1]
                    dve.wait_ge(s_xn[s], norm(g, "D2"))
                    link(g, dve.tensor_tensor(zg[s][:], z[s][:], R("g1").unsqueeze(1).to_broadcast((128, SPS, D)),
                                              ALU.mult))
                    dve.wait_ge(s_xnb[s], g + 1)
                    dve.tensor_tensor(y[s][:], zg[s][:], xnb[s][:], ALU.add).then_inc(s_y[s], 1)
                elif kind == "M" and g is not None:
                    _, s, L, u = st
                    i, q = divmod(u, NQ)
                    n, nk = m_unit(g, s, L, u), KEYS[L]
                    dve.wait_ge(s_sc, n + 1)
                    dve.tensor_reduce(negmax[s][:, i, q:NH:NQ], scb[u % 2][:, 0:NT * nk].rearrange(
                        "p (t k) -> p t k", t=NT), X_AXIS, ALU.max, negate=True).then_inc(s_scread, 1)
                    if q == NQ - 1:
                        dve.wait_ge(s_scread, n + 3)
                        link(g, dve.tensor_copy(m8[s][:, i, :, 0], negmax[s][:, i, :]))
                        dve.tensor_tensor(m8[s][:, i, :, 1], negmax[s][:, i, :], m8[s][:, i, :, 0], ALU.subtract
                                          ).then_inc(s_m8[s], 1)
                elif kind == "hop" and g is not None:
                    hop_step(g, st[1], st[2])
                elif kind == "moe_start" and gm is not None:
                    moe_at[0] = 0
                    dve.wait_ge(s_accinit, gm + 1)
                    dve.tensor_copy(acc[:].rearrange("p i d -> p (i d)"), db[:]).then_inc(s_acc, 1)
                    dve.wait_ge(s_acc, gm * (E1 + 1) + 2)
                elif kind == "moe" and gm is not None:
                    k = moe_at[0]
                    moe_at[0] += 1
                    if k and k % CH == 0:
                        take_up(gm, k // CH - 1)
                elif kind == "moe_end" and gm is not None:
                    take_up(gm, E1 - 1)
                    for i in range(GROUP):
                        ins = dve.bn_stats(statsF[:, i, :], acc[:, i, :])
                    link_moe(gm, ins)
                    dve.sem_inc(s_passed[0], 1)
                    for i in range(GROUP):
                        ins = dve.bn_aggr(mvF[:, i, :], statsF[:, i, :])
                    link_moe(gm, ins)
                    dve.tensor_scalar(veF[:], mvF[:, :, 1], EPS, None, ALU.add).then_inc(s_veF, 1)
                    dve.wait_ge(s_rstdF, gm + 1)
                    for i in range(GROUP):
                        last = dve.tensor_scalar(zF[:, i, :], acc[:, i, :], mvF[:, i, 0:1], rstdF[:, i:i + 1],
                                                 ALU.subtract, ALU.mult)
                    last.then_inc(s_zF, 1)

            def counted(g, gm, st):
                if st is STEPS[0]:
                    att[0] = moe[0] = 0
                step(g, gm, st)
                if st is STEPS[-1]:
                    assert g is None or att[0] == ATT_LINKS, att
                    assert gm is None or moe[0] == MOE_LINKS, moe

            for s in range(NS):
                dve.memset(v9[s][:, :, :, HD:VW], 1.0)
                dve.memset(v9C[s][:, :, :, HD:VW], 1.0)
                dve.memset(m8[s][:], 0.0)
                dve.memset(hlC[s][:], 0.0)
            dve.memset(onesrow[:], 1.0).then_inc(s_init_dve, 1)
            dve.wait_ge(s_init_dve, 1)
            for s in range(NS):
                dve.sem_inc(s_read[s], 1)
            dve.sem_inc(s_scread, 2)
            dve.sem_inc(s_acc, 1)
            dve.wait_ge(s_const, N_CONST * 16)
            dve.tensor_copy(w1hi[:], w1f[:]).then_inc(s_w1hi, 1)
            dve.wait_ge(s_w1hi, 1)
            dve.tensor_tensor(w1lo[:], w1f[:], w1hi[:], ALU.subtract).then_inc(s_w1lo, 1)
            run(dve, counted)

        @block.gpsimd
        def _(pool):
            pool.memset(neghalf[:], -0.5).then_inc(s_init_pool, 1)
            pool.wait_ge(s_init_pool, 1)
            pool.sem_inc(s_exp, 2)
            pool.sem_inc(s_pv, 4)
            pool.sem_inc(s_relu, 1)
            pool.sem_inc(s_down, 2)
            pool.sem_inc(s_store, 1)
            pool.wait_ge(s_const, N_CONST * 16)

            def step(g, gm, st):
                kind = st[0]
                if kind == "ln1" and g is not None:
                    _, s, N = st
                    pool.wait_ge(s_ve[s], norm(g, N))
                    pool.tensor_tensor(rstd[s][:], ve[s][:], neghalf[:, 0:SPS], ALU.pow).then_inc(s_rstd[s], 1)
                elif kind == "stack" and g is not None and st[2] == "D":
                    s = st[1]
                    pool.wait_ge(s_xn[s], norm(g, "D"))
                    pool.tensor_tensor(xnb[s][:], xnD[s][:], R("b1").unsqueeze(1).to_broadcast((128, SPS, D)),
                                       ALU.add).then_inc(s_xnb[s], 1)
                elif kind == "y" and g is not None:
                    s = st[1]
                    pool.wait_ge(s_y[s], g + 1)
                    pool.wait_ge(s_read[s], read(g, "C.wo"))
                    pool.tensor_tensor(xy[s][:], xs[s][:], y[s][:], ALU.add).then_inc(c_pool, 1)
                    pool.wait_ge(c_pool, NS * g + s + 1)
                    after(pool, s_outb, g)
                    pool.tensor_tensor(base[s][:], xy[s][:], R("b2").unsqueeze(1).to_broadcast((128, SPS, D)),
                                       ALU.add).then_inc(s_base[s], 1)
                elif kind == "moe_end" and gm is not None:
                    pool.wait_ge(s_veF, gm + 1)
                    pool.tensor_tensor(rstdF[:], veF[:], neghalf[:], ALU.pow).then_inc(s_rstdF, 1)
                    pool.wait_ge(s_zF, gm + 1)
                    pool.tensor_tensor(zgF[:], zF[:], R("g2").unsqueeze(1).to_broadcast((128, GROUP, D)),
                                       ALU.mult).then_inc(c_poolF, 1)
                    pool.wait_ge(c_poolF, gm + 1)
                    pool.wait_ge(s_store, 16 * gm + 1)
                    for s in range(NS):
                        pool.wait_ge(s_base[s], gm + 1)
                        a, b = s * SPS, (s + 1) * SPS
                        last = pool.tensor_tensor(outb[:, a:b, :], zgF[:, a:b, :], base[s][:], ALU.add)
                    last.then_inc(s_outb, 1)

            run(pool, step)


def kernel(**inputs):
    import concourse.bacc as bacc
    from concourse.bass_utils import run_bass_kernel_spmd

    a = {n: np.asarray(v) for n, v in inputs.items()}
    f32 = np.float32

    swap = np.arange(D).reshape(NH, 2, HD // 2)[:, ::-1].reshape(D)
    inv_freq = (1.0 / (10000.0 ** (np.arange(0, HD, 2, dtype=f32) / f32(HD)))).astype(f32)
    angle = np.outer(np.arange(T, dtype=f32), inv_freq).astype(f32)
    cos = np.tile(np.cos(angle).T, (2 * NH, 1)).astype(f32)
    sin = np.concatenate([-np.sin(angle).T, np.sin(angle).T])
    sin = np.tile(sin, (NH, 1)).astype(f32)
    low = np.tri(T, dtype=bool)
    mask = np.where(low, 0.0, MASKED).astype(np.float16)
    ones = np.zeros((128, NT * W), np.float16)
    ones[[i for i in range(32) if i % 8 < 2]] = 1.0
    half = {"ident16": np.eye(128, dtype=np.float16), "maskS": np.tile(mask, (1, NT)),
            "maskST": np.tile(mask.T, (1, NT)), "ones": ones, "zeros": np.zeros((128, NT * W), np.float16)}

    def tri(E, upper):
        m = np.triu(np.ones((E, E), f32), 1) if upper else np.tril(np.ones((E, E), f32), -1)
        return np.tile(m.reshape(1, -1), (128, SPS))

    w0 = np.stack([a[f"L0_ffn_W{n}"] for n in "qkv"], 2).transpose(1, 0, 2, 3).reshape(D, -1)
    b0 = np.stack([a[f"L0_ffn_b{n}"] for n in "qkv"], 0).transpose(2, 0, 1).reshape(D, -1)

    def heads(w):
        return w.transpose(1, 0, 2).reshape(D, D)

    pack = {"ident": np.eye(128, dtype=f32), "w0": w0, "wg1": a["L0_ffn_Wg1"], "wo0": a["L0_ffn_Wo"],
            "wq": a["L1_xattn_Wq"].T, "wqp": a["L1_xattn_Wq"][swap].T,
            "wk": a["L1_xattn_Wk"].T, "wkp": a["L1_xattn_Wk"][swap].T,
            "wv": a["L1_xattn_Wv"].T, "wo1": a["L1_xattn_Wo"].T,
            "dq": heads(a["L1_ffn_Wq"]), "dk": heads(a["L1_ffn_Wk"]), "dv": heads(a["L1_ffn_Wv"]),
            "wg2": a["L0_ffn_Wg2"], "gate": a["L1_ffn_gate_W"], "bg1": a["L0_ffn_bg1"].reshape(-1, 1), "b0": b0,
            "b1": a["L1_ffn_b1"].reshape(UNITS, 128).T, "cos": cos, "sin": sin,
            "triL0": tri(E0, False), "triU0": tri(E0, True), "triL1": tri(E1, False), "triU1": tri(E1, True)}
    rows = {"g1": a["L1_ffn_ln1_g"], "b1": a["L1_ffn_ln1_b"], "g2": a["L1_ffn_ln2_g"], "b2": a["L1_ffn_ln2_b"],
            "bg2": a["L0_ffn_bg2"]}
    arrays = {
        "x": a["x"], "ctx": a["ctx_1024"],
        "pack": np.concatenate([pack[n] for n, _ in PACK], 1),
        "rows": np.concatenate([rows[n] for n, _ in ROWS]).reshape(1, -1),
        "half": np.concatenate([half[n] for n, _ in HALF], 1),
        "w1": a["L1_ffn_W1"].transpose(1, 0, 2).reshape(D, -1),
        "w2": a["L1_ffn_W2"].reshape(UNITS, 128, D).transpose(1, 0, 2),
        "b2": a["L1_ffn_b2"], "bo": a["L0_ffn_bo"].reshape(1, -1),
    }
    arrays = {n: np.ascontiguousarray(v) for n, v in arrays.items()}
    nc = bacc.Bacc("TRN2", target_bir_lowering=False, num_devices=1)
    args = {n: nc.dram_tensor(f"in_{n}", v.shape, mybir.dt.from_np(v.dtype), kind="ExternalInput").ap()
            for n, v in arrays.items()}
    out = nc.dram_tensor("out", (B, T, D), F32, kind="ExternalOutput").ap()
    build(nc, out=out, **args)
    r = run_bass_kernel_spmd(nc, [{f"in_{n}": v for n, v in arrays.items()}], core_ids=[0])
    return r.results[0]["out"]
```

```python
from contextlib import ExitStack

import numpy as np

import concourse.bass as bass
from concourse import mybir

F32 = mybir.dt.float32
F16 = mybir.dt.float16
ALU = mybir.AluOpType
ACT = mybir.ActivationFunctionType
X_AXIS = mybir.AxisListType.X

B, T, D, NKC = 16, 128, 128, 77
NH, HD = 16, 8
E0, E1, FF = 4, 8, 512
GROUP = 4
NS = 2
SPS = GROUP // NS
W = SPS * T
NG = B // GROUP
CH = FF // 128
UNITS = E1 * CH
NQ = 4
NT = NH // NQ
VW = HD + 1
EPS = 1e-5
LAYERS = ("B", "C", "D")
KEYS = {"B": T, "C": NKC, "D": T}
SCALE = {"B": HD ** -0.5, "C": HD ** -0.5, "D": D ** -0.5}
MASKED = -60000.0

PACK = (("ident", 128), ("w0", E0 * 3 * D), ("wg1", D), ("wo0", D), ("wq", D), ("wqp", D), ("wk", D), ("wkp", D),
        ("wv", D), ("wo1", D), ("dq", D), ("dk", D), ("dv", D), ("wg2", E0), ("gate", E1), ("bg1", 1),
        ("b0", 3 * E0), ("b1", UNITS), ("cos", T), ("sin", T), ("triL0", SPS * E0 * E0), ("triU0", SPS * E0 * E0),
        ("triL1", SPS * E1 * E1), ("triU1", SPS * E1 * E1))
PACK_AT, PACK_W = {}, 0
for _n, _w in PACK:
    PACK_AT[_n] = (PACK_W, PACK_W + _w)
    PACK_W += _w
ROWS = (("g1", D), ("b1", D), ("g2", D), ("b2", D), ("bg2", E0))
ROWS_AT, ROWS_W = {}, 0
for _n, _w in ROWS:
    ROWS_AT[_n] = (ROWS_W, ROWS_W + _w)
    ROWS_W += _w

HALF = (("ident16", 128), ("maskS", NT * T), ("maskST", NT * T), ("ones", NT * W), ("zeros", NT * W))
HALF_AT, HALF_W = {}, 0
for _n, _w in HALF:
    HALF_AT[_n] = (HALF_W, HALF_W + _w)
    HALF_W += _w

HOPS = ("ctxT", "A.xT", "A.s", "A.pT", "A.o", "C.k", "C.v",
        "B.xT", "B.hid", "B.lg", "B.qk", "B.v", "B.mt", "B.pv", "B.oT", "B.wo",
        "C.xT", "C.q", "C.mt", "C.pv", "C.oT", "C.wo",
        "D.xT", "D.qk", "D.v", "D.mt", "D.pv", "D.yT", "D.lg", "D.cT")
NORMS = ("A", "B", "C", "D", "D2")
UPP = SPS * NQ
LAG = 3
LOW_DVE = (1, 3, 5)
LOW_POOL = tuple(u for u in range(UPP) if u not in LOW_DVE)
STACK_DMAS = 3 * NT + 1
MAX_DMAS = NT


def schedule():
    fill = ("fill",)

    def hops(s, *names):
        return [("hop", s, n) for n in names]

    def norm(s, n):
        return [("ln1", s, n), ("ln2", s, n)]

    def begin(s):
        return (hops(s, "ctxT") + norm(s, "A") + hops(s, "A.xT", "A.s", "A.pT", "A.o", "C.k", "C.v"))

    def head(s, L):
        if L == "C":
            return norm(s, "C") + hops(s, "C.xT", "C.q") + [("stack", s, "C")]
        return norm(s, "D") + hops(s, "D.xT", "D.qk") + [("stack", s, "D")] + hops(s, "D.v")

    def tail(s, L):
        if L == "D":
            return hops(s, "D.pv") + norm(s, "D2") + [("y", s)] + hops(s, "D.yT", "D.lg", "D.cT")
        return hops(s, L + ".pv", L + ".oT", L + ".wo")

    def exps(s, L, fills=True):
        out = []
        for u in range(UPP + LAG):
            if u < UPP:
                out.append(("E", s, L, u))
            if u >= LAG:
                out.append(("PV", s, L, u - LAG))
            if fills and u in (1, 4, 7, 9):
                out.append(fill)
        return out

    def maxima(s, L):
        return [("M", s, L, u) for u in range(UPP)] + hops(s, L + ".mt")

    def mixed(a, b):
        keyed = [((n + 0.5) / len(a), 0, x) for n, x in enumerate(a)]
        keyed += [((n + 0.5) / len(b), 1, x) for n, x in enumerate(b)]
        return [x for _, _, x in sorted(keyed, key=lambda k: k[:2])]

    steps = [("load", s) for s in range(NS)]
    steps += mixed([("prev", x) for x in exps(1, "D", False)], begin(0))
    steps += mixed([("prev", x) for x in tail(1, "D")], norm(0, "B") + hops(0, "B.xT", "B.hid", "B.lg"))
    steps += [("moe_start",), fill] + hops(0, "B.qk") + [("stack", 0, "B"), fill] + hops(0, "B.v")
    steps += mixed(begin(1), [fill] * 4)
    steps += mixed(maxima(0, "B"), norm(1, "B") + hops(1, "B.xT", "B.hid", "B.lg"))
    steps += [fill] + hops(1, "B.qk") + [("stack", 1, "B")] + hops(1, "B.v")
    order = [(s, L) for L in LAYERS for s in range(NS)]
    for n, (s, L) in enumerate(order[:-1]):
        steps += exps(s, L)
        if (s, L) == (0, "D"):
            steps += [("moe_end",)]
        other = tail(s, L) + (head(s, LAYERS[LAYERS.index(L) + 1]) if L != "D" else [])
        both = maxima(*order[n + 1])
        steps += mixed(both, other[:6]) + [fill] * (L != "D") + other[6:]
    places, n, out = steps.count(fill), 0, []
    for x in steps:
        if x == fill:
            out += [("moe",)] * (UNITS * (n + 1) // places - UNITS * n // places)
            n += 1
        else:
            out.append(x)
    assert out.count(("moe",)) == UNITS
    return out


STEPS = schedule()


def numbered(kind):
    turns = {}
    for step in STEPS:
        if step[0] == kind and step[1:3] not in turns:
            turns[step[1:3]] = len(turns)
    if (1, "D") not in turns:
        turns[1, "D"] = len(turns)
    return turns


M_TURN, E_TURN = numbered("M"), numbered("E")
N_CONST = 7
ATT_LINKS = 100
PREV_LINKS = 13
MOE_LINKS = 2
PASSES = len(M_TURN)


def build(nc, x, ctx, pack, rows, half, w1, w2, b2, bo, out):
    with ExitStack() as stack:
        def sb(name, shape, dt=F32):
            return stack.enter_context(nc.sbuf_tensor(name, shape, dt))

        def sem(name):
            return stack.enter_context(nc.semaphore(name))

        def per_stream(make, name, *a):
            return [make(f"{name}{s}", *a) for s in range(NS)]

        pk = sb("pk", [128, PACK_W])
        rw = sb("rw", [128, ROWS_W])
        hf = sb("hf", [128, HALF_W], F16)
        w1f = sb("w1f", [128, UNITS * 128])
        w1hi = sb("w1hi", [128, UNITS * 128], F16)
        w1lo = sb("w1lo", [128, UNITS * 128], F16)
        w2f = sb("w2f", [128, UNITS, D])
        b2f = sb("b2f", [E1, D])
        bof = sb("bof", [1, D])
        onesrow = sb("onesrow", [1, T])
        neghalf = sb("neghalf", [128, GROUP])

        def P(name, rows_=128):
            a, b = PACK_AT[name]
            return pk[0:rows_, a:b]

        def R(name):
            a, b = ROWS_AT[name]
            return rw[:, a:b]

        def H(name):
            a, b = HALF_AT[name]
            return hf[:, a:b]

        xin = per_stream(sb, "xin", [128, SPS, D])
        cin = per_stream(sb, "cin", [NKC, SPS, D])
        ctxT = per_stream(sb, "ctxT", [128, SPS * NKC])
        xs = per_stream(sb, "xs", [128, SPS, D])
        stats = per_stream(sb, "stats", [128, SPS, 6])
        mv = per_stream(sb, "mv", [128, SPS, 2])
        ve = per_stream(sb, "ve", [128, SPS])
        rstd = per_stream(sb, "rstd", [128, SPS])
        xn = per_stream(sb, "xn", [128, SPS, D])
        xnT = per_stream(sb, "xnT", [128, W])
        nmA = per_stream(sb, "nmA", [128, SPS])
        sumA = per_stream(sb, "sumA", [128, SPS])
        rinvA = per_stream(sb, "rinvA", [128, SPS])
        pA = per_stream(sb, "pA", [128, SPS, NKC])
        pAT = per_stream(sb, "pAT", [NKC, W])
        pooled = per_stream(sb, "pooled", [128, SPS])
        hid = per_stream(sb, "hid", [128, SPS])
        hidw = per_stream(sb, "hidw", [128, SPS, 128])
        lg = per_stream(sb, "lg", [128, SPS * E1])
        lmax = per_stream(sb, "lmax", [128, SPS])
        lsub = per_stream(sb, "lsub", [128, SPS * E1])
        lexp = per_stream(sb, "lexp", [128, SPS * E1])
        pair = per_stream(sb, "pair", [128, SPS * E1 * E1])
        above = per_stream(sb, "above", [128, SPS * E1 * E1])
        tied = per_stream(sb, "tied", [128, SPS * E1 * E1])
        rank = per_stream(sb, "rank", [128, SPS * E1])
        picked = per_stream(sb, "picked", [128, SPS * E1])
        psumw = per_stream(sb, "psumw", [128, SPS])
        gw = per_stream(sb, "gw", [128, SPS, E0])
        wc = per_stream(sb, "wc", [128, SPS, 3 * D])
        bmix = per_stream(sb, "bmix", [128, 3, SPS, E0])
        bqkv = per_stream(sb, "bqkv", [128, 3 * SPS])
        qkf = per_stream(sb, "qkf", [128, 2, W])
        rope1 = per_stream(sb, "rope1", [128, W])
        rope2 = per_stream(sb, "rope2", [128, W])
        hl = per_stream(sb, "hl", [128, 4, W], F16)
        hlC = per_stream(sb, "hlC", [128, 4, W], F16)
        qk = per_stream(sb, "qk", [128, 2, NT, W], F16)
        vhi = per_stream(sb, "vhi", [128, SPS, NH, VW], F16)
        vlo = per_stream(sb, "vlo", [128, SPS, NH, VW], F16)
        vhiC = per_stream(sb, "vhiC", [NKC, SPS, NH, VW], F16)
        vloC = per_stream(sb, "vloC", [NKC, SPS, NH, VW], F16)
        negmax = per_stream(sb, "negmax", [128, SPS, NH])
        m8 = per_stream(sb, "m8", [128, SPS, NH, 8], F16)
        mT = per_stream(sb, "mT", [128, W], F16)
        rden = per_stream(sb, "rden", [128, SPS * NH])
        on = per_stream(sb, "on", [128, SPS, D])
        oT = per_stream(sb, "oT", [128, W])
        xnD = per_stream(sb, "xnD", [128, SPS, D])
        xnb = per_stream(sb, "xnb", [128, SPS, D])
        z = per_stream(sb, "z", [128, SPS, D])
        zg = per_stream(sb, "zg", [128, SPS, D])
        y = per_stream(sb, "y", [128, SPS, D])
        xy = per_stream(sb, "xy", [128, SPS, D])
        base = per_stream(sb, "base", [128, SPS, D])
        yT = per_stream(sb, "yT", [128, W])
        combT = per_stream(sb, "combT", [E1, W])
        probs = sb("probs", [128, 4, NT * T])
        phi = sb("phi", [128, 4, NT * T], F16)
        plo = sb("plo", [128, 4, NT * T], F16)
        yhi = sb("yhi", [128, GROUP * T], F16)
        ylo = sb("ylo", [128, GROUP * T], F16)
        comb = sb("comb", [128, GROUP, E1])
        hT = sb("hT", [128, 2, GROUP * T])
        acc = sb("acc", [128, GROUP, D])
        statsF = sb("statsF", [128, GROUP, 6])
        mvF = sb("mvF", [128, GROUP, 2])
        veF = sb("veF", [128, GROUP])
        rstdF = sb("rstdF", [128, GROUP])
        zF = sb("zF", [128, GROUP, D])
        zgF = sb("zgF", [128, GROUP, D])
        outb = sb("outb", [128, GROUP, D])

        scb = [stack.enter_context(nc.psum_tensor(f"scb{i}", [128, NT * T], F32)) for i in range(2)]
        stb = [stack.enter_context(nc.psum_tensor(f"stb{i}", [128, NT * T], F32)) for i in range(2)]
        mb = [stack.enter_context(nc.psum_tensor(f"mb{i}", [128, 512], F32)) for i in range(NS)]
        ub = stack.enter_context(nc.psum_tensor("ub", [128, GROUP * T], F32))
        db = stack.enter_context(nc.psum_tensor("db", [128, GROUP * D], F32))

        s_const = sem("s_const")
        s_w1hi, s_w1lo = sem("s_w1hi"), sem("s_w1lo")
        s_init_dve, s_init_pool = sem("s_init_dve"), sem("s_init_pool")
        s_ones = sem("s_ones")
        s_loaded = per_stream(sem, "s_loaded")
        s_hop = per_stream(sem, "s_hop")
        s_read = per_stream(sem, "s_read")
        s_ve = per_stream(sem, "s_ve")
        s_rstd = per_stream(sem, "s_rstd")
        s_xn = per_stream(sem, "s_xn")
        s_nmA = per_stream(sem, "s_nmA")
        s_hidw = per_stream(sem, "s_hidw")
        s_lsub = per_stream(sem, "s_lsub")
        s_lexp = per_stream(sem, "s_lexp")
        s_wc = per_stream(sem, "s_wc")
        s_qkf = per_stream(sem, "s_qkf")
        s_hi = per_stream(sem, "s_hi")
        s_hl = per_stream(sem, "s_hl")
        s_stack = per_stream(sem, "s_stack")
        s_vhi = per_stream(sem, "s_vhi")
        s_m8 = per_stream(sem, "s_m8")
        s_max = per_stream(sem, "s_max")
        s_on = per_stream(sem, "s_on")
        s_xnb = per_stream(sem, "s_xnb")
        s_y = per_stream(sem, "s_y")
        s_base = per_stream(sem, "s_base")
        s_comb = per_stream(sem, "s_comb")
        s_sc, s_scread = sem("s_sc"), sem("s_scread")
        s_st, s_exp, s_pv = sem("s_st"), sem("s_exp"), sem("s_pv")
        s_lodve, s_lopool = sem("s_lodve"), sem("s_lopool")
        s_y16 = sem("s_y16")
        s_up, s_relu, s_down = sem("s_up"), sem("s_relu"), sem("s_down")
        s_accinit, s_acc = sem("s_accinit"), sem("s_acc")
        s_veF, s_rstdF, s_zF = sem("s_veF"), sem("s_rstdF"), sem("s_zF")
        s_outb, s_store = sem("s_outb"), sem("s_store")
        s_passed = per_stream(sem, "s_passed")
        c_dve = sem("c_dve")
        c_moe = sem("c_moe")
        c_pool, c_poolF = sem("c_pool"), sem("c_poolF")

        def after(eng, s, value):
            if not (isinstance(value, int) and value <= 0):
                eng.wait_ge(s, value)

        def hop(g, name):
            return g * len(HOPS) + HOPS.index(name) + 1

        def read(g, name):
            return hop(g, name) + 1

        def layer(g, L, per=1):
            return (g * len(LAYERS) + LAYERS.index(L)) * per

        def norm(g, N):
            return g * len(NORMS) + NORMS.index(N) + 1

        def m_unit(g, s, L, u):
            return (g * PASSES + M_TURN[s, L]) * UPP + u

        def e_unit(g, s, L, u):
            return (g * PASSES + E_TURN[s, L]) * UPP + u

        def low_unit(g, s, L, u, units):
            return (g * PASSES + E_TURN[s, L]) * len(units) + units.index(u)

        def values(s, L):
            return (vhiC[s], vloC[s]) if L == "C" else (vhi[s], vlo[s])

        def value_heads(t):
            return t[:, :, :, 0:HD].rearrange("p i h e -> p (i h) e")

        def bank_heads(bank, L):
            return bank[0:KEYS[L], 0:W].rearrange("p (n e) -> p n e", e=HD)

        def low_part(eng, g, s, L, u, done):
            eng.wait_ge(s_exp, e_unit(g, s, L, u) + 3)
            nk = KEYS[L]
            eng.tensor_tensor(plo[0:nk, u % 4, :], probs[0:nk, u % 4, :], phi[0:nk, u % 4, :], ALU.subtract
                              ).then_inc(done, 1)

        def run(eng, step):
            def once(g, gm, before):
                for st in STEPS:
                    if st[0] != "prev":
                        step(g, gm, st)
                    elif before is not None:
                        step(before, None, st[1])

            once(0, None, None)
            with eng.Fori(1, NG) as g:
                once(g, g - 1, g - 1)
            once(None, NG - 1, NG - 1)

        block = stack.enter_context(nc.Block())

        @block.sync
        def _(sp):
            for dst, src in ((pk, pack), (hf, half), (w1f, w1), (w2f, w2), (b2f, b2), (bof, bo)):
                sp.dma_start(dst[:], src).then_inc(s_const, 16)
            sp.dma_start(rw[:], rows.partition_broadcast(128)).then_inc(s_const, 16)
            sp.wait_ge(s_const, N_CONST * 16)
            for s in range(NS):
                sp.dma_start(qk[s][3:128:4, 1, :, :], H("ones")[0:32].rearrange("p (t w) -> p t w", t=NT)
                             ).then_inc(s_ones, 16)

            def step(g, gm, st):
                kind = st[0]
                if kind == "load" and g is not None:
                    s = st[1]
                    after(sp, s_read[s], read(g - 1, "A.o") if not isinstance(g, int) or g else 0)
                    sp.sem_inc(s_passed[1], 1)
                    b0 = g * GROUP + s * SPS
                    sp.dma_start(xin[s][:], x[bass.ds(b0, SPS)].rearrange("b t d -> t b d")
                                 ).then_inc(s_loaded[s], 16)
                    sp.dma_start(cin[s][:], ctx[bass.ds(b0, SPS)].rearrange("b t d -> t b d")
                                 ).then_inc(s_loaded[s], 16)
                elif kind == "stack" and g is not None:
                    _, s, L = st
                    if L != "B":
                        sp.wait_ge(s_st, e_unit(g, s, LAYERS[LAYERS.index(L) - 1], UPP - 1) + 1)
                    elif not isinstance(g, int):
                        sp.wait_ge(s_st, e_unit(g - 1, s, "D", UPP - 1) + 1)
                    sp.sem_inc(s_passed[1], 1)
                    sp.wait_ge(s_hl[s], layer(g, L) + 1)
                    src = hlC[s] if L == "C" else hl[s]
                    for t in range(NT):
                        rows_ = slice(32 * t, 32 * t + 32)
                        for r, pick in enumerate((src[rows_, 0:4:2, :], src[rows_, 0:4:3, :], src[rows_, 1:3, :])):
                            sp.dma_start(qk[s][r:128:4, :, t, :], pick).then_inc(s_stack[s], 16)
                    sp.dma_start(qk[s][3:128:4, 0, :, :], H("zeros")[0:32].rearrange("p (t w) -> p t w", t=NT)
                                 ).then_inc(s_stack[s], 16)
                elif kind == "hop" and g is not None and st[2].endswith("mt"):
                    _, s, h = st
                    sp.wait_ge(s_read[s], read(g, h))
                    for t in range(NT):
                        sp.dma_start(qk[s][3:128:4, 0, t, :], mT[s][32 * t:32 * t + 32, :]
                                     ).then_inc(s_max[s], 16)
                elif kind == "moe_end" and gm is not None:
                    sp.wait_ge(s_outb, gm + 2)
                    sp.sem_inc(s_passed[1], 1)
                    sp.dma_start(out[bass.ds(gm * GROUP, GROUP)].rearrange("b t d -> t b d"), outb[:]
                                 ).then_inc(s_store, 16)

            run(sp, step)
            sp.wait_ge(s_store, 1 + 16 * NG)

        @block.tensor
        def _(pe):
            mm = pe.matmul
            ident, ident16 = P("ident"), H("ident16")

            def hop_step(g, s, h):
                bank = mb[s]
                pe.wait_ge(s_read[s], hop(g, h))
                if h == "ctxT":
                    pe.wait_ge(s_loaded[s], 32 * (g + 1))
                    for i in range(SPS):
                        last = pe.transpose(bank[:, i * NKC:(i + 1) * NKC], cin[s][:, i, :], P("ident", NKC)[:, 0:NKC])
                elif h in ("A.xT", "B.xT", "C.xT", "D.xT"):
                    N = h[0]
                    pe.wait_ge(s_xn[s], norm(g, N))
                    src = xnD[s] if N == "D" else xn[s]
                    for i in range(SPS):
                        last = pe.transpose(bank[:, i * T:(i + 1) * T], src[:, i, :], ident)
                elif h == "A.s":
                    for i in range(SPS):
                        last = mm(bank[:, i * NKC:(i + 1) * NKC], xnT[s][:, i * T:(i + 1) * T],
                                  ctxT[s][:, i * NKC:(i + 1) * NKC], start=True, stop=True)
                elif h == "A.pT":
                    for i in range(SPS):
                        last = pe.transpose(bank[0:NKC, i * T:(i + 1) * T], pA[s][:, i, :], ident)
                elif h == "A.o":
                    for i in range(SPS):
                        last = mm(bank[:, i * D:(i + 1) * D], pAT[s][:, i * T:(i + 1) * T], cin[s][:, i, :],
                                  start=True, stop=True)
                elif h == "C.k":
                    mm(bank[:, 0:SPS * NKC], P("wk"), ctxT[s][:], start=True, stop=True)
                    last = mm(bank[:, 256:256 + SPS * NKC], P("wkp"), ctxT[s][:], start=True, stop=True)
                elif h == "C.v":
                    for i in range(SPS):
                        last = mm(bank[0:NKC, i * D:(i + 1) * D], ctxT[s][:, i * NKC:(i + 1) * NKC], P("wv"),
                                  start=True, stop=True)
                elif h == "B.hid":
                    last = mm(bank[:, 0:SPS], P("wg1"), pooled[s][:], start=True, stop=True)
                elif h == "B.lg":
                    pe.wait_ge(s_hidw[s], g + 1)
                    for i in range(SPS):
                        last = mm(bank[:, i * E0:(i + 1) * E0], hidw[s][:, i, :], P("wg2"), start=True, stop=True)
                elif h == "B.qk":
                    pe.wait_ge(s_wc[s], g + 1)
                    for n in range(2):
                        for i in range(SPS):
                            last = mm(bank[:, n * W + i * T:n * W + (i + 1) * T], wc[s][:, i, n * D:(n + 1) * D],
                                      xnT[s][:, i * T:(i + 1) * T], start=True, stop=True)
                elif h == "B.v":
                    for i in range(SPS):
                        last = mm(bank[:, i * D:(i + 1) * D], xnT[s][:, i * T:(i + 1) * T],
                                  wc[s][:, i, 2 * D:3 * D], start=True, stop=True)
                elif h in ("C.q", "D.qk"):
                    a, b = ("wq", "wqp") if h == "C.q" else ("dq", "dk")
                    mm(bank[:, 0:W], P(a), xnT[s][:], start=True, stop=True)
                    last = mm(bank[:, W:2 * W], P(b), xnT[s][:], start=True, stop=True)
                elif h == "D.v":
                    for i in range(SPS):
                        last = mm(bank[:, i * D:(i + 1) * D], xnT[s][:, i * T:(i + 1) * T], P("dv"),
                                  start=True, stop=True)
                elif h.endswith("mt"):
                    pe.wait_ge(s_m8[s], layer(g, h[0], SPS) + SPS)
                    half_bank = bank[:].bitcast(F16)
                    for i in range(SPS):
                        last = pe.transpose(half_bank[:, i * T:(i + 1) * T],
                                            m8[s][:, i, :, :].rearrange("p h e -> p (h e)"), ident16)
                elif h.endswith("oT"):
                    pe.wait_ge(s_on[s], layer(g, h[0]) + 1)
                    for i in range(SPS):
                        last = pe.transpose(bank[:, i * T:(i + 1) * T], on[s][:, i, :], ident)
                elif h.endswith("wo"):
                    for i in range(SPS):
                        last = mm(bank[:, i * D:(i + 1) * D], oT[s][:, i * T:(i + 1) * T],
                                  P("wo0" if h[0] == "B" else "wo1"), start=True, stop=h[0] == "C")
                        if h[0] == "B":
                            last = mm(bank[:, i * D:(i + 1) * D], onesrow[:], bof[:], start=False, stop=True)
                elif h == "D.yT":
                    pe.wait_ge(s_y[s], g + 1)
                    for i in range(SPS):
                        last = pe.transpose(bank[:, i * T:(i + 1) * T], y[s][:, i, :], ident)
                elif h == "D.lg":
                    for i in range(SPS):
                        last = mm(bank[:, i * E1:(i + 1) * E1], yT[s][:, i * T:(i + 1) * T], P("gate"),
                                  start=True, stop=True)
                elif h == "D.cT":
                    pe.wait_ge(s_comb[s], g + 1)
                    for i in range(SPS):
                        last = pe.transpose(bank[0:E1, i * T:(i + 1) * T], comb[:, s * SPS + i, :], ident)
                last.then_inc(s_hop[s], 1)

            def stack_rows(s, n, q, t, i, width):
                return qk[s][32 * q:32 * q + 32, n, t, i * T:i * T + width]

            def weighted(g, s, L, u):
                i, q = divmod(u, NQ)
                if u == 0:
                    pe.wait_ge(s_read[s], hop(g, L + ".pv"))
                pe.wait_ge(s_exp, e_unit(g, s, L, u) + 3)
                if u in LOW_DVE:
                    pe.wait_ge(s_lodve, low_unit(g, s, L, u, LOW_DVE) + 1)
                else:
                    pe.wait_ge(s_lopool, low_unit(g, s, L, u, LOW_POOL) + 1)
                nk = KEYS[L]
                v_hi, v_lo = values(s, L)
                for t in range(NT):
                    h = NQ * t + q
                    o = mb[s][:, (i * NH + h) * VW:(i * NH + h + 1) * VW]
                    high, low = (p[0:nk, u % 4, t * T:(t + 1) * T] for p in (phi, plo))
                    mm(o, high, v_hi[0:nk, i, h, :], start=True, stop=False)
                    mm(o, high, v_lo[0:nk, i, h, :], start=False, stop=False)
                    last = mm(o, low, v_hi[0:nk, i, h, :], start=False, stop=True)
                last.then_inc(s_pv, 1)

            def down(gm, k):
                e, c = divmod(k, CH)
                if c == 0:
                    pe.wait_ge(s_acc, gm * (E1 + 1) + e + 2)
                pe.wait_ge(s_relu, gm * UNITS + k + 2)
                for i in range(GROUP):
                    last = mm(db[:, i * D:(i + 1) * D], hT[:, k % 2, i * T:(i + 1) * T], w2f[:, k, :],
                              start=c == 0 and i == 0, stop=c == CH - 1, skip_group_check=True)
                last.then_inc(s_down, 1)

            moe_at = [0]

            def step(g, gm, st):
                kind = st[0]
                if kind == "hop" and g is not None and not st[2].endswith("pv"):
                    hop_step(g, st[1], st[2])
                elif kind == "M" and g is not None:
                    _, s, L, u = st
                    i, q = divmod(u, NQ)
                    n, nk = m_unit(g, s, L, u), KEYS[L]
                    if u == 0:
                        pe.wait_ge(s_stack[s], (layer(g, L) + 1) * 16 * STACK_DMAS)
                    pe.wait_ge(s_scread, n + 1)
                    bank = scb[u % 2]
                    for t in range(NT):
                        last = mm(bank[:, t * nk:(t + 1) * nk], stack_rows(s, 0, q, t, i, T),
                                  stack_rows(s, 1, q, t, i, nk), start=L != "D" or t == 0, stop=L != "D")
                    if L == "D":
                        last = mm(bank[:], ident16, H("maskS"), start=False, stop=True)
                    last.then_inc(s_sc, 1)
                elif kind == "E" and g is not None:
                    _, s, L, u = st
                    i, q = divmod(u, NQ)
                    n, nk = e_unit(g, s, L, u), KEYS[L]
                    if u == 0:
                        pe.wait_ge(s_max[s], (layer(g, L) + 1) * 16 * MAX_DMAS)
                    pe.wait_ge(s_exp, n + 1)
                    bank = stb[u % 2]
                    for t in range(NT):
                        last = mm(bank[0:nk, t * T:(t + 1) * T], stack_rows(s, 1, q, t, i, nk),
                                  stack_rows(s, 0, q, t, i, T), start=L != "D" or t == 0, stop=L != "D")
                    if L == "D":
                        last = mm(bank[:], ident16, H("maskST"), start=False, stop=True)
                    last.then_inc(s_st, 1)
                elif kind == "PV" and g is not None:
                    weighted(g, *st[1:])
                elif kind == "moe_start" and gm is not None:
                    moe_at[0] = 0
                    pe.wait_ge(s_acc, gm * (E1 + 1) + 1)
                    for i in range(GROUP):
                        s = i // SPS
                        if i % SPS == 0:
                            pe.wait_ge(s_read[s], read(gm, "D.cT"))
                        last = mm(db[:, i * D:(i + 1) * D], combT[s][:, (i % SPS) * T:(i % SPS + 1) * T], b2f[:],
                                  start=True, stop=True)
                    last.then_inc(s_accinit, 1)
                    pe.wait_ge(s_y16, NS * (gm + 1))
                elif kind == "moe" and gm is not None:
                    k = moe_at[0]
                    moe_at[0] += 1
                    pe.wait_ge(s_relu, gm * UNITS + k + 1)
                    a, b = k * 128, (k + 1) * 128
                    mm(ub[:], w1hi[:, a:b], yhi[:], start=True, stop=False)
                    mm(ub[:], w1hi[:, a:b], ylo[:], start=False, stop=False)
                    mm(ub[:], w1lo[:, a:b], yhi[:], start=False, stop=True).then_inc(s_up, 1)
                    if k:
                        down(gm, k - 1)
                elif kind == "moe_end" and gm is not None:
                    down(gm, UNITS - 1)

            pe.wait_ge(s_const, N_CONST * 16)
            pe.wait_ge(s_w1lo, 1)
            pe.wait_ge(s_w1hi, 1)
            pe.wait_ge(s_init_dve, 1)
            pe.wait_ge(s_init_pool, 1)
            pe.wait_ge(s_ones, 16 * NS)
            run(pe, step)

        @block.scalar
        def _(act):
            moe_at = [0]

            def hop_step(g, s, h):
                bank = mb[s]
                if h not in ("ctxT", "A.xT", "A.s", "A.pT", "C.v", "B.xT", "B.hid", "B.lg", "B.qk", "B.v", "B.mt",
                             "C.xT", "C.mt", "C.oT", "D.xT", "D.qk", "D.v", "D.mt", "D.yT", "D.lg"):
                    return
                if h in ("B.lg", "D.lg"):
                    n = SPS * (E0 if h == "B.lg" else E1)
                    act.wait_ge(s_lsub[s], 2 * g + (1 if h == "B.lg" else 2))
                    act.activation(lexp[s][:, 0:n], lsub[s][:, 0:n], ACT.Exp).then_inc(s_lexp[s], 1)
                    return
                if h == "B.qk":
                    act.wait_ge(s_qkf[s], g + 1)
                    act.activation(hl[s][:, 0:4:2, :], qkf[s][:], ACT.Copy).then_inc(s_hi[s], 1)
                    return
                act.wait_ge(s_hop[s], hop(g, h))
                if h == "A.s":
                    act.wait_ge(s_nmA[s], g + 1)
                    for i in range(SPS):
                        last = act.activation(pA[s][:, i, :], bank[:, i * NKC:(i + 1) * NKC], ACT.Exp,
                                              bias=nmA[s][:, i:i + 1], accum_out=sumA[s][:, i:i + 1])
                elif h == "ctxT":
                    last = act.activation(ctxT[s][:], bank[:, 0:SPS * NKC], ACT.Copy)
                elif h == "B.xT":
                    for i in range(SPS):
                        last = act.activation(xnT[s][:, i * T:(i + 1) * T], bank[:, i * T:(i + 1) * T], ACT.Copy,
                                              accum_out=pooled[s][:, i:i + 1])
                elif h in ("A.xT", "C.xT", "D.xT"):
                    last = act.activation(xnT[s][:], bank[:, 0:W], ACT.Copy)
                elif h == "A.pT":
                    last = act.activation(pAT[s][:], bank[0:NKC, 0:W], ACT.Copy)
                elif h == "B.hid":
                    last = act.activation(hid[s][:], bank[:, 0:SPS], ACT.Relu, bias=P("bg1"), scale=1.0 / T)
                elif h in ("B.v", "D.v", "C.v"):
                    act.activation(value_heads(values(s, h[0])[0]), bank_heads(bank, h[0]), ACT.Copy
                                   ).then_inc(s_vhi[s], 1)
                    return
                elif h.endswith("mt"):
                    last = act.activation(mT[s][:], bank[:].bitcast(F16)[:, 0:W], ACT.Copy)
                elif h == "C.oT":
                    last = act.activation(oT[s][:], bank[:, 0:W], ACT.Copy)
                elif h == "D.qk":
                    act.activation(hl[s][:, 0:4:2, :], bank[:].rearrange("p (n w) -> p n w", n=2), ACT.Copy
                                   ).then_inc(s_hi[s], 1)
                    return
                elif h == "D.yT":
                    last = act.activation(yT[s][:], bank[:, 0:W], ACT.Copy)
                last.then_inc(s_read[s], 1)

            def step(g, gm, st):
                kind = st[0]
                if kind == "hop" and g is not None:
                    hop_step(g, st[1], st[2])
                elif kind == "E" and g is not None:
                    _, s, L, u = st
                    n, nk = e_unit(g, s, L, u), KEYS[L]
                    act.wait_ge(s_st, n + 1)
                    act.wait_ge(s_pv, n + 1)
                    for p in (phi, probs):
                        last = act.activation(p[0:nk, u % 4, :], stb[u % 2][0:nk, :], ACT.Exp, scale=SCALE[L])
                    last.then_inc(s_exp, 1)
                elif kind == "moe_start":
                    moe_at[0] = 0
                elif kind == "moe" and gm is not None:
                    k = moe_at[0]
                    moe_at[0] += 1
                    act.wait_ge(s_up, gm * UNITS + k + 1)
                    act.wait_ge(s_down, gm * UNITS + k + 1)
                    act.activation(hT[:, k % 2, :], ub[:], ACT.Relu, bias=P("b1")[:, k:k + 1]).then_inc(s_relu, 1)

            act.wait_ge(s_const, N_CONST * 16)
            act.wait_ge(s_init_dve, 1)
            run(act, step)

        @block.vector
        def _(dve):
            att = [0]
            base_links = [0]
            moe = [0]
            moe_at = [0]

            def link(g, ins):
                att[0] += 1
                ins.then_inc(c_dve, 1)
                dve.wait_ge(c_dve, base_links[0] + att[0])

            def link_moe(gm, ins):
                moe[0] += 1
                ins.then_inc(c_moe, 1)
                dve.wait_ge(c_moe, gm * MOE_LINKS + moe[0])

            def top2(g, s, bank, E, dst, bias, triL, triU, turn):
                n = SPS * E

                def v3(t):
                    return t[:, 0:n].rearrange("p (i e) -> p i e", i=SPS)

                lg3, sub3, exp3 = v3(lg[s]), v3(lsub[s]), v3(lexp[s])
                pr4 = pair[s][:, 0:n * E].rearrange("p (i e f) -> p i e f", i=SPS, e=E)
                src = bank[:, 0:n].rearrange("p (i e) -> p i e", i=SPS)
                if bias is not None:
                    ins = dve.tensor_tensor(lg3, src, bias.unsqueeze(1).to_broadcast((128, SPS, E)), ALU.add)
                else:
                    ins = dve.tensor_copy(lg3, src)
                ins.then_inc(s_read[s], 1)
                dve.wait_ge(s_read[s], read(g, "B.lg" if E == E0 else "D.lg"))
                link(g, dve.tensor_reduce(lmax[s][:], lg3, X_AXIS, ALU.max))
                dve.tensor_tensor(sub3, lg3, lmax[s][:].unsqueeze(2).to_broadcast((128, SPS, E)),
                                  ALU.subtract).then_inc(s_lsub[s], 1)
                for i in range(SPS):
                    ins = dve.tensor_tensor(pr4[:, i], lg3[:, i].unsqueeze(1).to_broadcast((128, E, E)),
                                            lg3[:, i].unsqueeze(2).to_broadcast((128, E, E)), ALU.subtract)
                link(g, ins)
                dve.scalar_tensor_tensor(out=above[s][:, 0:n * E], in0=pair[s][:, 0:n * E], scalar=0.0, in1=triU,
                                         op0=ALU.is_gt, op1=ALU.mult)
                link(g, dve.scalar_tensor_tensor(out=tied[s][:, 0:n * E], in0=pair[s][:, 0:n * E], scalar=0.0,
                                                 in1=triL, op0=ALU.is_ge, op1=ALU.mult))
                link(g, dve.tensor_tensor(pair[s][:, 0:n * E], above[s][:, 0:n * E], tied[s][:, 0:n * E], ALU.add))
                link(g, dve.tensor_reduce(rank[s][:, 0:n], pair[s][:, 0:n * E].rearrange("p (n f) -> p n f", f=E),
                                          X_AXIS, ALU.add))
                dve.wait_ge(s_lexp[s], 2 * g + turn)
                link(g, dve.scalar_tensor_tensor(out=picked[s][:, 0:n], in0=rank[s][:, 0:n], scalar=2.0,
                                                 in1=lexp[s][:, 0:n], op0=ALU.is_lt, op1=ALU.mult))
                link(g, dve.tensor_reduce(psumw[s][:], v3(picked[s]), X_AXIS, ALU.add))
                link(g, dve.reciprocal(lmax[s][:], psumw[s][:]))
                return dve.tensor_tensor(dst, v3(picked[s]), lmax[s][:].unsqueeze(2).to_broadcast((128, SPS, E)),
                                         ALU.mult)

            def rope(g, s, h, n, hi, lo):
                bank = mb[s]
                dve.wait_ge(s_hop[s], hop(g, h))

                def v3(t):
                    return t[:, 0:SPS * n].rearrange("p (i w) -> p i w", i=SPS)

                cos = P("cos")[:, 0:n].unsqueeze(1).to_broadcast((128, SPS, n))
                sin = P("sin")[:, 0:n].unsqueeze(1).to_broadcast((128, SPS, n))
                dve.tensor_tensor(v3(rope1[s]), v3(bank), cos, ALU.mult)
                dve.tensor_tensor(v3(rope2[s]), bank[:, 256:256 + SPS * n].rearrange("p (i w) -> p i w", i=SPS), sin,
                                  ALU.mult).then_inc(s_read[s], 1)
                dve.wait_ge(s_read[s], read(g, h))
                link(g, dve.tensor_tensor(qkf[s][:, 0, 0:SPS * n], rope1[s][:, 0:SPS * n], rope2[s][:, 0:SPS * n],
                                          ALU.add))
                link(g, dve.tensor_copy(hi, v3(qkf[s][:, 0, :])))
                return dve.tensor_tensor(lo, v3(qkf[s][:, 0, :]), hi, ALU.subtract)

            def hop_step(g, s, h):
                bank = mb[s]
                halves = bank[:].rearrange("p (n w) -> p n w", n=2)
                if h == "A.s":
                    dve.wait_ge(s_hop[s], hop(g, h))
                    dve.tensor_reduce(nmA[s][:], bank[:, 0:SPS * NKC].rearrange("p (i k) -> p i k", i=SPS), X_AXIS,
                                      ALU.max, negate=True).then_inc(s_nmA[s], 1)
                elif h == "A.o":
                    dve.wait_ge(s_hop[s], hop(g, h))
                    link(g, dve.reciprocal(rinvA[s][:], sumA[s][:]))
                    after(dve, s_base[s], g)
                    for i in range(SPS):
                        last = dve.scalar_tensor_tensor(out=xs[s][:, i, :], in0=bank[:, i * D:(i + 1) * D],
                                                        scalar=rinvA[s][:, i:i + 1], in1=xin[s][:, i, :],
                                                        op0=ALU.mult, op1=ALU.add)
                    last.then_inc(s_read[s], 1)
                elif h == "C.k":
                    k4 = hlC[s][:, 2:4, :].rearrange("p n (i w) -> p n i w", i=SPS)
                    link(g, rope(g, s, h, NKC, k4[:, 0, :, 0:NKC], k4[:, 1, :, 0:NKC]))
                elif h == "C.q":
                    q4 = hlC[s][:, 0:2, :].rearrange("p n (i w) -> p n i w", i=SPS)
                    rope(g, s, h, T, q4[:, 0], q4[:, 1]).then_inc(s_hl[s], 1)
                elif h == "B.hid":
                    dve.wait_ge(s_read[s], read(g, h))
                    dve.tensor_copy(hidw[s][:], hid[s][:].unsqueeze(2).to_broadcast((128, SPS, 128))
                                    ).then_inc(s_hidw[s], 1)
                elif h == "B.lg":
                    dve.wait_ge(s_hop[s], hop(g, h))
                    link(g, top2(g, s, bank, E0, gw[s][:], R("bg2"), P("triL0"), P("triU0"), 1))
                    w0 = P("w0").rearrange("p (e w) -> p e w", e=E0)
                    for e in range(E0):
                        for i in range(SPS):
                            if e == 0:
                                ins = dve.tensor_scalar(wc[s][:, i, :], w0[:, e, :], gw[s][:, i, e:e + 1], None,
                                                        ALU.mult)
                            else:
                                ins = dve.scalar_tensor_tensor(out=wc[s][:, i, :], in0=w0[:, e, :],
                                                               scalar=gw[s][:, i, e:e + 1], in1=wc[s][:, i, :],
                                                               op0=ALU.mult, op1=ALU.add)
                        if e < E0 - 1:
                            link(g, ins)
                    ins.then_inc(s_wc[s], 1)
                    b0 = P("b0").rearrange("p (n e) -> p n e", n=3)
                    for n in range(3):
                        ins = dve.tensor_tensor(bmix[s][:, n], b0[:, n, :].unsqueeze(1).to_broadcast((128, SPS, E0)),
                                                gw[s][:], ALU.mult)
                    link(g, ins)
                    link(g, dve.tensor_reduce(bqkv[s][:], bmix[s][:].rearrange("p n i e -> p (n i) e"), X_AXIS,
                                              ALU.add))
                elif h == "B.qk":
                    dve.wait_ge(s_hop[s], hop(g, h))
                    dve.tensor_tensor(qkf[s][:].rearrange("p n (i w) -> p (n i) w", i=SPS),
                                      bank[:].rearrange("p (m w) -> p m w", w=T),
                                      bqkv[s][:, 0:2 * SPS].unsqueeze(2).to_broadcast((128, 2 * SPS, T)), ALU.add
                                      ).then_inc(s_qkf[s], 1)
                    dve.wait_ge(s_qkf[s], g + 1)
                    dve.sem_inc(s_read[s], 1)
                    dve.wait_ge(s_hi[s], 2 * g + 1)
                    dve.tensor_tensor(hl[s][:, 1:4:2, :], qkf[s][:], hl[s][:, 0:4:2, :], ALU.subtract
                                      ).then_inc(s_hl[s], 1)
                elif h == "D.qk":
                    dve.wait_ge(s_hi[s], 2 * g + 2)
                    link(g, dve.tensor_tensor(hl[s][:, 1:4:2, :], halves, hl[s][:, 0:4:2, :], ALU.subtract))
                    dve.sem_inc(s_hl[s], 1)
                    dve.sem_inc(s_read[s], 1)
                elif h in ("C.v", "B.v", "D.v"):
                    dve.wait_ge(s_vhi[s], 3 * g + 1 + ("C.v", "B.v", "D.v").index(h))
                    high, low = values(s, h[0])
                    dve.tensor_tensor(value_heads(low), bank_heads(bank, h[0]), value_heads(high), ALU.subtract
                                      ).then_inc(s_read[s], 1)
                elif h.endswith("pv"):
                    n = e_unit(g, s, h[0], UPP - 1)
                    dve.wait_ge(s_pv, n + 5)
                    o3 = bank[:, 0:SPS * NH * VW].rearrange("p (n e) -> p n e", e=VW)
                    link(g, dve.reciprocal(rden[s][:].unsqueeze(2), o3[:, :, HD:VW]))
                    dve.tensor_tensor(on[s][:].rearrange("p i (h e) -> p (i h) e", e=HD), o3[:, :, 0:HD],
                                      rden[s][:].unsqueeze(2).to_broadcast((128, SPS * NH, HD)), ALU.mult
                                      ).then_inc(s_on[s], 1)
                    dve.wait_ge(s_on[s], layer(g, h[0]) + 1)
                    dve.sem_inc(s_hop[s], 1)
                    dve.sem_inc(s_read[s], 1)
                elif h == "B.oT":
                    dve.wait_ge(s_hop[s], hop(g, h))
                    for i in range(SPS):
                        last = dve.tensor_scalar(oT[s][:, i * T:(i + 1) * T], bank[:, i * T:(i + 1) * T],
                                                 bqkv[s][:, 2 * SPS + i:2 * SPS + i + 1], None, ALU.add)
                    last.then_inc(s_read[s], 1)
                elif h.endswith("wo"):
                    dve.wait_ge(s_hop[s], hop(g, h))
                    dve.tensor_tensor(xs[s][:].rearrange("p i d -> p (i d)"), bank[:, 0:W],
                                      xs[s][:].rearrange("p i d -> p (i d)"), ALU.add).then_inc(s_read[s], 1)
                elif h == "D.yT":
                    dve.wait_ge(s_read[s], read(g, h))
                    a, b = s * W, (s + 1) * W
                    link(g, dve.tensor_copy(yhi[:, a:b], yT[s][:]))
                    dve.tensor_tensor(ylo[:, a:b], yT[s][:], yhi[:, a:b], ALU.subtract).then_inc(s_y16, 1)
                elif h == "D.lg":
                    dve.wait_ge(s_hop[s], hop(g, h))
                    top2(g, s, bank, E1, comb[:, s * SPS:(s + 1) * SPS, :], None, P("triL1"), P("triU1"), 2
                         ).then_inc(s_comb[s], 1)
                elif h == "D.cT":
                    dve.wait_ge(s_hop[s], hop(g, h))
                    dve.tensor_copy(combT[s][:], bank[0:E1, 0:W]).then_inc(s_read[s], 1)

            def take_up(gm, e):
                dve.wait_ge(s_down, gm * UNITS + (e + 1) * CH + 2)
                for i in range(GROUP):
                    last = dve.scalar_tensor_tensor(out=acc[:, i, :], in0=db[:, i * D:(i + 1) * D],
                                                    scalar=comb[:, i, e:e + 1], in1=acc[:, i, :],
                                                    op0=ALU.mult, op1=ALU.add)
                last.then_inc(s_acc, 1)
                dve.wait_ge(s_acc, gm * (E1 + 1) + e + 3)

            def step(g, gm, st):
                kind = st[0]
                if kind == "ln1" and g is not None:
                    _, s, N = st
                    if N == "A":
                        dve.wait_ge(s_loaded[s], 32 * (g + 1))
                    elif N == "B":
                        dve.wait_ge(s_read[s], read(g, "A.o"))
                    elif N == "D2":
                        dve.wait_ge(s_on[s], layer(g, "D") + 1)
                    else:
                        dve.wait_ge(s_read[s], read(g, {"C": "B.wo", "D": "C.wo"}[N]))
                    src = {"A": xin, "D2": on}.get(N, xs)[s]
                    for i in range(SPS):
                        ins = dve.bn_stats(stats[s][:, i, :], src[:, i, :])
                    link(g, ins)
                    dve.sem_inc(s_passed[0], 1)
                    for i in range(SPS):
                        ins = dve.bn_aggr(mv[s][:, i, :], stats[s][:, i, :])
                    link(g, ins)
                    dve.tensor_scalar(ve[s][:], mv[s][:, :, 1], EPS, None, ALU.add).then_inc(s_ve[s], 1)
                elif kind == "ln2" and g is not None:
                    _, s, N = st
                    dve.wait_ge(s_rstd[s], norm(g, N))
                    src = {"A": xin, "D2": on}.get(N, xs)[s]
                    dst = {"D": xnD, "D2": z}.get(N, xn)[s]
                    for i in range(SPS):
                        last = dve.tensor_scalar(dst[:, i, :], src[:, i, :], mv[s][:, i, 0:1], rstd[s][:, i:i + 1],
                                                 ALU.subtract, ALU.mult)
                    last.then_inc(s_xn[s], 1)
                elif kind == "y" and g is not None:
                    s = st[1]
                    dve.wait_ge(s_xn[s], norm(g, "D2"))
                    link(g, dve.tensor_tensor(zg[s][:], z[s][:], R("g1").unsqueeze(1).to_broadcast((128, SPS, D)),
                                              ALU.mult))
                    dve.wait_ge(s_xnb[s], g + 1)
                    dve.tensor_tensor(y[s][:], zg[s][:], xnb[s][:], ALU.add).then_inc(s_y[s], 1)
                elif kind == "M" and g is not None:
                    _, s, L, u = st
                    i, q = divmod(u, NQ)
                    n, nk = m_unit(g, s, L, u), KEYS[L]
                    dve.wait_ge(s_sc, n + 1)
                    dve.tensor_reduce(negmax[s][:, i, q:NH:NQ], scb[u % 2][:, 0:NT * nk].rearrange(
                        "p (t k) -> p t k", t=NT), X_AXIS, ALU.max, negate=True).then_inc(s_scread, 1)
                    if q == NQ - 1:
                        dve.wait_ge(s_scread, n + 3)
                        link(g, dve.tensor_copy(m8[s][:, i, :, 0], negmax[s][:, i, :]))
                        dve.tensor_tensor(m8[s][:, i, :, 1], negmax[s][:, i, :], m8[s][:, i, :, 0], ALU.subtract
                                          ).then_inc(s_m8[s], 1)
                elif kind == "E" and g is not None:
                    _, s, L, u = st
                    if u - 1 in LOW_DVE:
                        low_part(dve, g, s, L, u - 1, s_lodve)
                elif kind == "hop" and g is not None:
                    hop_step(g, st[1], st[2])
                elif kind == "moe_start" and gm is not None:
                    moe_at[0] = 0
                    dve.wait_ge(s_accinit, gm + 1)
                    dve.tensor_copy(acc[:].rearrange("p i d -> p (i d)"), db[:]).then_inc(s_acc, 1)
                    dve.wait_ge(s_acc, gm * (E1 + 1) + 2)
                elif kind == "moe" and gm is not None:
                    k = moe_at[0]
                    moe_at[0] += 1
                    if k and k % CH == 0:
                        take_up(gm, k // CH - 1)
                elif kind == "moe_end" and gm is not None:
                    take_up(gm, E1 - 1)
                    for i in range(GROUP):
                        ins = dve.bn_stats(statsF[:, i, :], acc[:, i, :])
                    link_moe(gm, ins)
                    dve.sem_inc(s_passed[0], 1)
                    for i in range(GROUP):
                        ins = dve.bn_aggr(mvF[:, i, :], statsF[:, i, :])
                    link_moe(gm, ins)
                    dve.tensor_scalar(veF[:], mvF[:, :, 1], EPS, None, ALU.add).then_inc(s_veF, 1)
                    dve.wait_ge(s_rstdF, gm + 1)
                    for i in range(GROUP):
                        last = dve.tensor_scalar(zF[:, i, :], acc[:, i, :], mvF[:, i, 0:1], rstdF[:, i:i + 1],
                                                 ALU.subtract, ALU.mult)
                    last.then_inc(s_zF, 1)

            def counted(g, gm, st):
                if st is STEPS[0]:
                    it = g if g is not None else NG
                    moe[0] = 0
                    att[0] = PREV_LINKS if isinstance(g, int) and g == 0 else 0
                    base_links[0] = it * ATT_LINKS - PREV_LINKS
                step(g, gm, st)
                if st is STEPS[-1]:
                    assert g is None or att[0] == ATT_LINKS, att
                    assert gm is None or moe[0] == MOE_LINKS, moe

            for s in range(NS):
                for v_hi, v_lo in (values(s, "B"), values(s, "C")):
                    dve.memset(v_hi[:, :, :, HD:VW], 1.0)
                    dve.memset(v_lo[:, :, :, HD:VW], 0.0)
                dve.memset(m8[s][:], 0.0)
                dve.memset(hlC[s][:], 0.0)
            dve.memset(onesrow[:], 1.0).then_inc(s_init_dve, 1)
            dve.wait_ge(s_init_dve, 1)
            for s in range(NS):
                dve.sem_inc(s_read[s], 1)
            dve.sem_inc(s_scread, 2)
            dve.sem_inc(s_acc, 1)
            dve.wait_ge(s_const, N_CONST * 16)
            dve.tensor_copy(w1hi[:], w1f[:]).then_inc(s_w1hi, 1)
            dve.wait_ge(s_w1hi, 1)
            dve.tensor_tensor(w1lo[:], w1f[:], w1hi[:], ALU.subtract).then_inc(s_w1lo, 1)
            run(dve, counted)

        @block.gpsimd
        def _(pool):
            pool.memset(neghalf[:], -0.5).then_inc(s_init_pool, 1)
            pool.wait_ge(s_init_pool, 1)
            pool.sem_inc(s_exp, 2)
            pool.sem_inc(s_pv, 4)
            pool.sem_inc(s_relu, 1)
            pool.sem_inc(s_down, 2)
            pool.sem_inc(s_store, 1)
            pool.sem_inc(s_outb, 1)
            pool.wait_ge(s_const, N_CONST * 16)

            def step(g, gm, st):
                kind = st[0]
                if kind == "ln1" and g is not None:
                    _, s, N = st
                    pool.wait_ge(s_ve[s], norm(g, N))
                    pool.tensor_tensor(rstd[s][:], ve[s][:], neghalf[:, 0:SPS], ALU.pow).then_inc(s_rstd[s], 1)
                elif kind == "stack" and g is not None and st[2] == "D":
                    s = st[1]
                    pool.wait_ge(s_xn[s], norm(g, "D"))
                    pool.tensor_tensor(xnb[s][:], xnD[s][:], R("b1").unsqueeze(1).to_broadcast((128, SPS, D)),
                                       ALU.add).then_inc(s_xnb[s], 1)
                elif kind == "E" and g is not None and st[3] in LOW_POOL:
                    low_part(pool, g, *st[1:], s_lopool)
                elif kind == "y" and g is not None:
                    s = st[1]
                    pool.wait_ge(s_y[s], g + 1)
                    pool.wait_ge(s_read[s], read(g, "C.wo"))
                    pool.tensor_tensor(xy[s][:], xs[s][:], y[s][:], ALU.add).then_inc(c_pool, 1)
                    pool.wait_ge(c_pool, NS * g + s + 1)
                    pool.wait_ge(s_outb, g + 1)
                    pool.tensor_tensor(base[s][:], xy[s][:], R("b2").unsqueeze(1).to_broadcast((128, SPS, D)),
                                       ALU.add).then_inc(s_base[s], 1)
                elif kind == "moe_end" and gm is not None:
                    pool.wait_ge(s_veF, gm + 1)
                    pool.tensor_tensor(rstdF[:], veF[:], neghalf[:], ALU.pow).then_inc(s_rstdF, 1)
                    pool.wait_ge(s_zF, gm + 1)
                    pool.tensor_tensor(zgF[:], zF[:], R("g2").unsqueeze(1).to_broadcast((128, GROUP, D)),
                                       ALU.mult).then_inc(c_poolF, 1)
                    pool.wait_ge(c_poolF, gm + 1)
                    pool.wait_ge(s_store, 16 * gm + 1)
                    for s in range(NS):
                        pool.wait_ge(s_base[s], gm + 1)
                        a, b = s * SPS, (s + 1) * SPS
                        last = pool.tensor_tensor(outb[:, a:b, :], zgF[:, a:b, :], base[s][:], ALU.add)
                    last.then_inc(s_outb, 1)

            run(pool, step)


def kernel(**inputs):
    import concourse.bacc as bacc
    from concourse.bass_utils import run_bass_kernel_spmd

    a = {n: np.asarray(v) for n, v in inputs.items()}
    f32 = np.float32

    swap = np.arange(D).reshape(NH, 2, HD // 2)[:, ::-1].reshape(D)
    inv_freq = (1.0 / (10000.0 ** (np.arange(0, HD, 2, dtype=f32) / f32(HD)))).astype(f32)
    angle = np.outer(np.arange(T, dtype=f32), inv_freq).astype(f32)
    cos = np.tile(np.cos(angle).T, (2 * NH, 1)).astype(f32)
    sin = np.concatenate([-np.sin(angle).T, np.sin(angle).T])
    sin = np.tile(sin, (NH, 1)).astype(f32)
    low = np.tri(T, dtype=bool)
    mask = np.where(low, 0.0, MASKED).astype(np.float16)
    ones = np.zeros((128, NT * W), np.float16)
    ones[[i for i in range(32) if i % 8 < 2]] = 1.0
    half = {"ident16": np.eye(128, dtype=np.float16), "maskS": np.tile(mask, (1, NT)),
            "maskST": np.tile(mask.T, (1, NT)), "ones": ones, "zeros": np.zeros((128, NT * W), np.float16)}

    def tri(E, upper):
        m = np.triu(np.ones((E, E), f32), 1) if upper else np.tril(np.ones((E, E), f32), -1)
        return np.tile(m.reshape(1, -1), (128, SPS))

    w0 = np.stack([a[f"L0_ffn_W{n}"] for n in "qkv"], 2).transpose(1, 0, 2, 3).reshape(D, -1)
    b0 = np.stack([a[f"L0_ffn_b{n}"] for n in "qkv"], 0).transpose(2, 0, 1).reshape(D, -1)

    def heads(w):
        return w.transpose(1, 0, 2).reshape(D, D)

    pack = {"ident": np.eye(128, dtype=f32), "w0": w0, "wg1": a["L0_ffn_Wg1"], "wo0": a["L0_ffn_Wo"],
            "wq": a["L1_xattn_Wq"].T, "wqp": a["L1_xattn_Wq"][swap].T,
            "wk": a["L1_xattn_Wk"].T, "wkp": a["L1_xattn_Wk"][swap].T,
            "wv": a["L1_xattn_Wv"].T, "wo1": a["L1_xattn_Wo"].T,
            "dq": heads(a["L1_ffn_Wq"]), "dk": heads(a["L1_ffn_Wk"]), "dv": heads(a["L1_ffn_Wv"]),
            "wg2": a["L0_ffn_Wg2"], "gate": a["L1_ffn_gate_W"], "bg1": a["L0_ffn_bg1"].reshape(-1, 1), "b0": b0,
            "b1": a["L1_ffn_b1"].reshape(UNITS, 128).T, "cos": cos, "sin": sin,
            "triL0": tri(E0, False), "triU0": tri(E0, True), "triL1": tri(E1, False), "triU1": tri(E1, True)}
    rows = {"g1": a["L1_ffn_ln1_g"], "b1": a["L1_ffn_ln1_b"], "g2": a["L1_ffn_ln2_g"], "b2": a["L1_ffn_ln2_b"],
            "bg2": a["L0_ffn_bg2"]}
    arrays = {
        "x": a["x"], "ctx": a["ctx_1024"],
        "pack": np.concatenate([pack[n] for n, _ in PACK], 1),
        "rows": np.concatenate([rows[n] for n, _ in ROWS]).reshape(1, -1),
        "half": np.concatenate([half[n] for n, _ in HALF], 1),
        "w1": a["L1_ffn_W1"].transpose(1, 0, 2).reshape(D, -1),
        "w2": a["L1_ffn_W2"].reshape(UNITS, 128, D).transpose(1, 0, 2),
        "b2": a["L1_ffn_b2"], "bo": a["L0_ffn_bo"].reshape(1, -1),
    }
    arrays = {n: np.ascontiguousarray(v) for n, v in arrays.items()}
    nc = bacc.Bacc("TRN2", target_bir_lowering=False, num_devices=1)
    args = {n: nc.dram_tensor(f"in_{n}", v.shape, mybir.dt.from_np(v.dtype), kind="ExternalInput").ap()
            for n, v in arrays.items()}
    out = nc.dram_tensor("out", (B, T, D), F32, kind="ExternalOutput").ap()
    build(nc, out=out, **args)
    r = run_bass_kernel_spmd(nc, [{f"in_{n}": v for n, v in arrays.items()}], core_ids=[0])
    return r.results[0]["out"]
```

```python
from contextlib import ExitStack

import numpy as np

import concourse.bass as bass
from concourse import mybir

F32 = mybir.dt.float32
F16 = mybir.dt.float16
ALU = mybir.AluOpType
ACT = mybir.ActivationFunctionType
X_AXIS = mybir.AxisListType.X

B, T, D, NKC = 16, 128, 128, 77
NH, HD = 16, 8
E0, E1, FF = 4, 8, 512
GROUP = 4
NS = 2
LANES = 2 * NS
MOE = LANES
SPS = GROUP // NS
W = SPS * T
NG = B // GROUP
CH = FF // 128
UNITS = E1 * CH
NQ = 4
NT = NH // NQ
VW = HD + 1
EPS = 1e-5
KEYS = {"B": T, "C": NKC, "D": T}
SCALE = {"B": HD ** -0.5, "C": HD ** -0.5, "D": D ** -0.5}
MASKED = -60000.0

PACK = (("ident", 128), ("w0", E0 * 3 * D), ("wg1", D), ("wo0", D), ("wq", D), ("wqp", D), ("wk", D), ("wkp", D),
        ("wv", D), ("wo1", D), ("dq", D), ("dk", D), ("dv", D), ("wg2", E0), ("gate", E1), ("bg1", 1),
        ("b0", 3 * E0), ("ones", 1), ("b1", UNITS), ("cos", T), ("sin", T), ("triL0", SPS * E0 * E0), ("triU0", SPS * E0 * E0),
        ("triL1", SPS * E1 * E1), ("triU1", SPS * E1 * E1))
PACK_AT, PACK_W = {}, 0
for _n, _w in PACK:
    PACK_AT[_n] = (PACK_W, PACK_W + _w)
    PACK_W += _w
ROWS = (("g1", D), ("b1", D), ("g2", D), ("b2", D), ("bg2", E0))
ROWS_AT, ROWS_W = {}, 0
for _n, _w in ROWS:
    ROWS_AT[_n] = (ROWS_W, ROWS_W + _w)
    ROWS_W += _w

HALF = (("ident16", 128), ("maskS", NT * T), ("maskST", NT * T), ("pick", NT * 4 * 128))
HALF_AT, HALF_W = {}, 0
for _n, _w in HALF:
    HALF_AT[_n] = (HALF_W, HALF_W + _w)
    HALF_W += _w

HOPS = (("ctxT", "A.xT", "A.s", "A.pT", "A.o", "B.xT", "B.hid", "B.lg", "B.qk", "B.v", "B.mt", "C.k", "C.v",
         "B.pv", "B.oT", "B.wo"),
        ("C.xT", "C.q", "C.mt", "C.pv", "C.oT", "C.wo",
         "D.xT", "D.qk", "D.v", "D.mt", "D.pv", "D.yT", "D.lg", "D.cT"))
NORMS = (("A", "B"), ("C", "D", "D2"))
LAYERS = (("B",), ("C", "D"))
UPP = SPS * NQ
LOW_DVE = (1, 3, 5)
BANKS, RING = 3, 4
STACKINGS = 4
STACK_DVE = (1,)
MAX_DMAS = NT


def way(lane):
    def hops(*names):
        return [("hop", n) for n in names]

    def norm(n):
        return [("ln1", n), ("ln2", n)]

    def units(kind, L, n=UPP):
        return [(kind, L, u) for u in range(n)]

    if lane == MOE:
        return [("moe_start",)] + [("moe", n) for n in range(UNITS)] + [("moe_end",)]
    if lane < NS:
        steps = (hops("ctxT") + norm("A") + hops("A.xT", "A.s", "A.pT", "A.o") + norm("B")
                 + hops("B.xT", "B.hid", "B.lg", "B.qk") + units("stack", "B", STACKINGS) + hops("B.v")
                 + units("M", "B") + hops("B.mt", "C.k", "C.v") + units("E", "B") + hops("B.pv", "B.oT", "B.wo"))
    else:
        steps = (norm("C") + hops("C.xT", "C.q") + units("stack", "C", STACKINGS) + units("M", "C")
                 + hops("C.mt") + units("E", "C") + hops("C.pv", "C.oT", "C.wo")
                 + norm("D") + hops("D.xT", "D.qk") + units("stack", "D", STACKINGS) + hops("D.v")
                 + units("M", "D") + hops("D.mt") + units("E", "D") + hops("D.pv") + norm("D2") + [("y",)]
                 + hops("D.yT", "D.lg", "D.cT"))
    return [(st[0], lane) + st[1:] for st in steps]


ORDER = (
    "420103410431303013333023103l2103l02231ll0140v302v24v2v24lllvl31l40v3lvv432v4l23120lv2102413vl00v3320"
    "ll432v0l14vv20210v1221130423014241222242220341143241043044123l41021l32214lv2ll34v30v32vvl13400l0v3l1"
    "244l03v23ll3v03v03l33lv03lv1032v0v1lll2v1v1ll4v1v2l10v3lvl23vl023v32v3v3lv3lv30ll2llv12lv1lv1lv3223v"
    "332v3322v23124124212323442232234")
FIRST, AGE = (0, 0, 16, 4, 5), (0, 0, 0, 0, 1)
LATE = {"v": 0, "l": 0}


def schedule():
    steps = [(0, ("load", s)) for s in range(NS)]
    steps.append((1, ("skip",)))
    ways, at = [way(lane) for lane in range(MOE + 1)], list(FIRST)
    exps = []
    for c in ORDER:
        if c not in "vl":
            lane, n = int(c), at[int(c)]
            step = (AGE[lane] + (n >= FIRST[lane] > 0), ways[lane][n])
            steps.append(step)
            at[lane] = (n + 1) % len(ways[lane])
            if step[1][0] == "E":
                exps.append(step)
        else:
            steps.append(c)
    turn = {c: -LATE[c] for c in "vl"}
    for n, step in enumerate(steps):
        if step in ("v", "l"):
            age, unit = exps[turn[step]]
            steps[n] = (age + (turn[step] < 0), ({"v": "PV", "l": "low"}[step],) + unit[1:])
            turn[step] += 1
    return steps


STEPS = schedule()


def numbers():
    counts = {"bank": 0, "E": 0, "low dve": 0, "low pool": 0}
    table = [{} for _ in range(NG)]
    for it in range(NG + 2):
        before = dict(counts)
        for age, st in STEPS:
            if 0 <= it - age < NG and st[0] in ("stack", "M", "E", "moe", "skip", "low"):
                kinds = {"E": ("bank", "E"), "low": ("low dve" if st[-1] in LOW_DVE else "low pool",)
                         }.get(st[0], ("bank",))
                for kind in kinds:
                    table[it - age][(kind,) + st] = counts[kind]
                    counts[kind] += 1
        if it == 2:
            per = {kind: counts[kind] - before[kind] for kind in counts}
    return table, per


NUMBERS, PER_ITERATION = numbers()
SECOND = next(st for _, st in STEPS if st[0] == "ln1" and st[2] == "B")
SPLIT = next(st for _, st in STEPS if st[0] == "hop" and st[2] == "B.v")
N_CONST = 3
N_MOE = 3
LINKS = 102


def build(nc, x, ctx, pack, rows, half, w1, w2, b2, bo, out):
    with ExitStack() as stack:
        def sb(name, shape, dt=F32):
            return stack.enter_context(nc.sbuf_tensor(name, shape, dt))

        def sem(name):
            return stack.enter_context(nc.semaphore(name))

        def per_lane(make, name, *a):
            return [make(f"{name}{s}", *a) for s in range(LANES)]

        def first(make, name, *a):
            return [make(f"{name}{s}", *a) for s in range(NS)] + [None] * NS

        def second(make, name, *a):
            return [None] * NS + [make(f"{name}{s}", *a) for s in range(NS, LANES)]

        pk = sb("pk", [128, PACK_W])
        rw = sb("rw", [128, ROWS_W])
        hf = sb("hf", [128, HALF_W], F16)
        w1f = sb("w1f", [128, UNITS * 128])
        w1hi = sb("w1hi", [128, UNITS * 128], F16)
        w1lo = sb("w1lo", [128, UNITS * 128], F16)
        w2f = sb("w2f", [128, UNITS, D])
        b2f = sb("b2f", [E1, D])
        bof = sb("bof", [1, D])
        onesrow = sb("onesrow", [1, T])
        neghalf = sb("neghalf", [128, GROUP])

        def P(name, rows_=128):
            a, b = PACK_AT[name]
            return pk[0:rows_, a:b]

        def R(name):
            a, b = ROWS_AT[name]
            return rw[:, a:b]

        def H(name):
            a, b = HALF_AT[name]
            return hf[:, a:b]

        xin = first(sb, "xin", [128, SPS, D])
        cin = first(sb, "cin", [NKC, SPS, D])
        ctxT = first(sb, "ctxT", [128, SPS * NKC])
        xs = per_lane(sb, "xs", [128, SPS, D])
        xm = first(sb, "xm", [128, SPS, D])
        stats = per_lane(sb, "stats", [128, SPS, 6])
        mv = per_lane(sb, "mv", [128, SPS, 2])
        ve = per_lane(sb, "ve", [128, SPS])
        rstd = per_lane(sb, "rstd", [128, SPS])
        xn = per_lane(sb, "xn", [128, SPS, D])
        xnT = per_lane(sb, "xnT", [128, W])
        nmA = first(sb, "nmA", [128, SPS])
        sumA = first(sb, "sumA", [128, SPS])
        rinvA = first(sb, "rinvA", [128, SPS])
        pA = first(sb, "pA", [128, SPS, NKC])
        pAT = first(sb, "pAT", [NKC, W])
        pooled = first(sb, "pooled", [128, SPS])
        hid = first(sb, "hid", [128, SPS])
        hidw = first(sb, "hidw", [128, SPS, 128])
        lg = per_lane(sb, "lg", [128, SPS * E1])
        lmax = per_lane(sb, "lmax", [128, SPS])
        lsub = per_lane(sb, "lsub", [128, SPS * E1])
        lexp = per_lane(sb, "lexp", [128, SPS * E1])
        pair = per_lane(sb, "pair", [128, SPS * E1 * E1])
        above = per_lane(sb, "above", [128, SPS * E1 * E1])
        tied = per_lane(sb, "tied", [128, SPS * E1 * E1])
        rank = per_lane(sb, "rank", [128, SPS * E1])
        picked = per_lane(sb, "picked", [128, SPS * E1])
        psumw = per_lane(sb, "psumw", [128, SPS])
        gw = first(sb, "gw", [128, SPS, E0])
        wc = first(sb, "wc", [128, SPS, 3 * D])
        bmix = first(sb, "bmix", [128, 3, SPS, E0])
        bqkv = first(sb, "bqkv", [128, 3 * SPS])
        qkf = per_lane(sb, "qkf", [128, 2, W])
        rope1 = per_lane(sb, "rope1", [128, W])
        rope2 = per_lane(sb, "rope2", [128, W])
        hl = per_lane(sb, "hl", [128, 4, W], F16)
        hlC = first(sb, "hlC", [128, 4, W], F16)
        qk = per_lane(sb, "qk", [128, 2, NT, W], F16)
        vhi = per_lane(sb, "vhi", [128, SPS, NH, VW], F16)
        vlo = per_lane(sb, "vlo", [128, SPS, NH, VW], F16)
        vhiC = first(sb, "vhiC", [NKC, SPS, NH, VW], F16)
        vloC = first(sb, "vloC", [NKC, SPS, NH, VW], F16)
        negmax = per_lane(sb, "negmax", [128, SPS, NH])
        m8 = per_lane(sb, "m8", [128, SPS, NH, 8], F16)
        mT = per_lane(sb, "mT", [128, W], F16)
        rden = per_lane(sb, "rden", [128, SPS * NH])
        on = per_lane(sb, "on", [128, SPS, D])
        oT = per_lane(sb, "oT", [128, W])
        xnD = second(sb, "xnD", [128, SPS, D])
        xnb = second(sb, "xnb", [128, SPS, D])
        z = second(sb, "z", [128, SPS, D])
        zg = second(sb, "zg", [128, SPS, D])
        y = second(sb, "y", [128, SPS, D])
        xy = second(sb, "xy", [128, SPS, D])
        base = second(sb, "base", [128, SPS, D])
        yT = second(sb, "yT", [128, W])
        combT = second(sb, "combT", [E1, W])
        ring = RING * NT * T

        def in_ring(view):
            return view.rearrange("p (r w) -> p r w", r=RING)

        assert 2 * ring <= UNITS * 128
        probs = in_ring(w1f[:, 0:ring])
        phi = in_ring(w1f[:, ring:ring + ring // 2].bitcast(F16))
        plo = in_ring(w1f[:, ring + ring // 2:2 * ring].bitcast(F16))
        yhi = sb("yhi", [128, GROUP * T], F16)
        ylo = sb("ylo", [128, GROUP * T], F16)
        comb = sb("comb", [128, GROUP, E1])
        hT = sb("hT", [128, 2, GROUP * T])
        acc = sb("acc", [128, GROUP, D])
        statsF = sb("statsF", [128, GROUP, 6])
        mvF = sb("mvF", [128, GROUP, 2])
        veF = sb("veF", [128, GROUP])
        rstdF = sb("rstdF", [128, GROUP])
        zF = sb("zF", [128, GROUP, D])
        zgF = sb("zgF", [128, GROUP, D])
        outb = sb("outb", [128, GROUP, D])

        bk = [stack.enter_context(nc.psum_tensor(f"bk{i}", [128, NT * T], F32)) for i in range(BANKS)]
        mb = [stack.enter_context(nc.psum_tensor(f"mb{i}", [128, 512], F32)) for i in range(LANES)]
        db = stack.enter_context(nc.psum_tensor("db", [128, GROUP * D], F32))

        s_first, s_const, s_moe = sem("s_first"), sem("s_const"), sem("s_moe")
        s_w1hi, s_w1lo = sem("s_w1hi"), sem("s_w1lo")
        s_init_dve, s_init_pool = sem("s_init_dve"), sem("s_init_pool")
        s_loaded = first(sem, "s_loaded")
        s_hop = per_lane(sem, "s_hop")
        s_read = per_lane(sem, "s_read")
        s_ve = per_lane(sem, "s_ve")
        s_rstd = per_lane(sem, "s_rstd")
        s_xn = per_lane(sem, "s_xn")
        s_nmA = first(sem, "s_nmA")
        s_hidw = first(sem, "s_hidw")
        s_lsub = per_lane(sem, "s_lsub")
        s_lexp = per_lane(sem, "s_lexp")
        s_wc = first(sem, "s_wc")
        s_qkf = first(sem, "s_qkf")
        s_hi = per_lane(sem, "s_hi")
        s_hl = per_lane(sem, "s_hl")
        s_vhi = per_lane(sem, "s_vhi")
        s_m8 = per_lane(sem, "s_m8")
        s_max = per_lane(sem, "s_max")
        s_on = per_lane(sem, "s_on")
        s_xnb = second(sem, "s_xnb")
        s_y = second(sem, "s_y")
        s_base = second(sem, "s_base")
        s_comb = second(sem, "s_comb")
        s_full = [sem(f"s_full{i}") for i in range(BANKS)]
        s_free = [sem(f"s_free{i}") for i in range(BANKS)]
        s_exp, s_pv = sem("s_exp"), sem("s_pv")
        s_lodve, s_lopool = sem("s_lodve"), sem("s_lopool")
        s_y16 = sem("s_y16")
        s_down = sem("s_down")
        s_accinit, s_acc = sem("s_accinit"), sem("s_acc")
        s_veF, s_rstdF, s_zF = sem("s_veF"), sem("s_rstdF"), sem("s_zF")
        s_outb, s_store = sem("s_outb"), sem("s_store")
        s_passed = [sem("s_passed0"), sem("s_passed1")]
        c_dve = sem("c_dve")
        c_pool, c_poolF = sem("c_pool"), sem("c_poolF")

        def after(eng, s, value):
            if not (isinstance(value, int) and value <= 0):
                eng.wait_ge(s, value)

        def turn(lists, g, name):
            items = next(l for l in lists if name in l)
            return g * len(items) + items.index(name) + 1

        def hop(g, name):
            return turn(HOPS, g, name)

        def read(g, name):
            return hop(g, name) + 1

        def layer(g, L):
            return turn(LAYERS, g, L)

        def norm(g, N):
            return turn(NORMS, g, N)

        def values(s, L):
            return (vhiC[s % NS], vloC[s % NS]) if L == "C" else (vhi[s], vlo[s])

        def value_heads(t):
            return t[:, :, :, 0:HD].rearrange("p i h e -> p (i h) e")

        def bank_heads(bank, L):
            return bank[0:KEYS[L], 0:W].rearrange("p (n e) -> p n e", e=HD)

        def stack_part(s, u):
            return qk[s][:, u // 2, u % 2 * 2:u % 2 * 2 + 2, :].rearrange("p t w -> p (t w)")

        def exp_unit(count, s, L, u):
            unit = ("E", s, L, u)
            return count("E", unit, RING)[0], count("E", unit)[1]

        def low_part(eng, count, st, done):
            _, s, L, u = st
            p, n = exp_unit(count, s, L, u)
            eng.wait_ge(s_exp, n + 1)
            nk = KEYS[L]
            eng.tensor_tensor(plo[0:nk, p, :], probs[0:nk, p, :], phi[0:nk, p, :], ALU.subtract
                              ).then_inc(done, 1)

        def run(eng, step, ready, begin=None):
            def once(it):
                if begin:
                    begin(it)
                for age, st in STEPS:
                    if isinstance(it, int) and not 0 <= it - age < NG:
                        continue
                    if isinstance(it, int) and it == 0 and st == SECOND:
                        ready()

                    def count(kind, unit, ring=1):
                        if isinstance(it, int):
                            n = NUMBERS[it - age][(kind,) + unit]
                            return n % ring, n // ring
                        n, per = NUMBERS[2 - age][(kind,) + unit], PER_ITERATION[kind]
                        assert NUMBERS[3 - age][(kind,) + unit] == n + per and per % ring == 0
                        return n % ring, it * (per // ring) + (n // ring - 2 * (per // ring))

                    step(it - age if age else it, count, st)

            for it in (0, 1):
                once(it)
            with eng.Fori(2, NG) as it:
                once(it)
            for it in (NG, NG + 1):
                once(it)

        block = stack.enter_context(nc.Block())

        @block.sync
        def _(sp):
            a, b = PACK_AT["ident"]
            sp.dma_start(pk[:, a:b], pack[:, a:b]).then_inc(s_first, 16)
            sp.dma_start(rw[:], rows.partition_broadcast(128)).then_inc(s_first, 16)

            def ready():
                sp.dma_start(pk[:, b:], pack[:, b:]).then_inc(s_const, 16)
                for dst, src in ((hf, half), (bof, bo)):
                    sp.dma_start(dst[:], src).then_inc(s_const, 16)
                for dst, src in ((w1f, w1), (w2f, w2), (b2f, b2)):
                    sp.dma_start(dst[:], src).then_inc(s_moe, 16)

            def step(g, count, st):
                kind = st[0]
                if kind == "load":
                    s = st[1]
                    after(sp, s_read[s], read(g - 1, "A.o"))
                    sp.sem_inc(s_passed[1], 1)
                    b0 = g * GROUP + s * SPS
                    sp.dma_start(xin[s][:], x[bass.ds(b0, SPS)].rearrange("b t d -> t b d")
                                 ).then_inc(s_loaded[s], 16)
                    sp.dma_start(cin[s][:], ctx[bass.ds(b0, SPS)].rearrange("b t d -> t b d")
                                 ).then_inc(s_loaded[s], 16)
                elif kind == "hop" and st[2].endswith("mt"):
                    _, s, h = st
                    sp.wait_ge(s_read[s], read(g, h))
                    for t in range(NT):
                        sp.dma_start(qk[s][3:128:4, 0, t, :], mT[s][32 * t:32 * t + 32, :]
                                     ).then_inc(s_max[s], 16)
                elif kind == "moe_end":
                    sp.wait_ge(s_outb, g + 2)
                    sp.sem_inc(s_passed[1], 1)
                    sp.dma_start(out[bass.ds(g * GROUP, GROUP)].rearrange("b t d -> t b d"), outb[:]
                                 ).then_inc(s_store, 16)

            run(sp, step, ready)
            sp.wait_ge(s_store, 1 + 16 * NG)

        @block.tensor
        def _(pe):
            mm = pe.matmul
            ident, ident16 = P("ident"), H("ident16")

            def hop_step(g, s, h):
                bank = mb[s]
                pe.wait_ge(s_read[s], hop(g, h))
                if h == "ctxT":
                    pe.wait_ge(s_loaded[s], 32 * (g + 1))
                    for i in range(SPS):
                        last = pe.transpose(bank[:, i * NKC:(i + 1) * NKC], cin[s][:, i, :], P("ident", NKC)[:, 0:NKC])
                elif h in ("A.xT", "B.xT", "C.xT", "D.xT"):
                    N = h[0]
                    pe.wait_ge(s_xn[s], norm(g, N))
                    src = xnD[s] if N == "D" else xn[s]
                    for i in range(SPS):
                        last = pe.transpose(bank[:, i * T:(i + 1) * T], src[:, i, :], ident)
                elif h == "A.s":
                    for i in range(SPS):
                        last = mm(bank[:, i * NKC:(i + 1) * NKC], xnT[s][:, i * T:(i + 1) * T],
                                  ctxT[s][:, i * NKC:(i + 1) * NKC], start=True, stop=True)
                elif h == "A.pT":
                    for i in range(SPS):
                        last = pe.transpose(bank[0:NKC, i * T:(i + 1) * T], pA[s][:, i, :], ident)
                elif h == "A.o":
                    for i in range(SPS):
                        last = mm(bank[:, i * D:(i + 1) * D], pAT[s][:, i * T:(i + 1) * T], cin[s][:, i, :],
                                  start=True, stop=True)
                elif h == "C.k":
                    mm(bank[:, 0:SPS * NKC], P("wk"), ctxT[s][:], start=True, stop=True)
                    last = mm(bank[:, 256:256 + SPS * NKC], P("wkp"), ctxT[s][:], start=True, stop=True)
                elif h == "C.v":
                    for i in range(SPS):
                        last = mm(bank[0:NKC, i * D:(i + 1) * D], ctxT[s][:, i * NKC:(i + 1) * NKC], P("wv"),
                                  start=True, stop=True)
                elif h == "B.hid":
                    last = mm(bank[:, 0:SPS], P("wg1"), pooled[s][:], start=True, stop=True)
                elif h == "B.lg":
                    pe.wait_ge(s_hidw[s], g + 1)
                    for i in range(SPS):
                        last = mm(bank[:, i * E0:(i + 1) * E0], hidw[s][:, i, :], P("wg2"), start=True, stop=True)
                elif h == "B.qk":
                    pe.wait_ge(s_wc[s], g + 1)
                    for n in range(2):
                        for i in range(SPS):
                            last = mm(bank[:, n * W + i * T:n * W + (i + 1) * T], wc[s][:, i, n * D:(n + 1) * D],
                                      xnT[s][:, i * T:(i + 1) * T], start=True, stop=True)
                elif h == "B.v":
                    for i in range(SPS):
                        last = mm(bank[:, i * D:(i + 1) * D], xnT[s][:, i * T:(i + 1) * T],
                                  wc[s][:, i, 2 * D:3 * D], start=True, stop=True)
                elif h in ("C.q", "D.qk"):
                    a, b = ("wq", "wqp") if h == "C.q" else ("dq", "dk")
                    mm(bank[:, 0:W], P(a), xnT[s][:], start=True, stop=True)
                    last = mm(bank[:, W:2 * W], P(b), xnT[s][:], start=True, stop=True)
                elif h == "D.v":
                    for i in range(SPS):
                        last = mm(bank[:, i * D:(i + 1) * D], xnT[s][:, i * T:(i + 1) * T], P("dv"),
                                  start=True, stop=True)
                elif h.endswith("mt"):
                    pe.wait_ge(s_m8[s], layer(g, h[0]) * SPS)
                    half_bank = bank[:].bitcast(F16)
                    for i in range(SPS):
                        last = pe.transpose(half_bank[:, i * T:(i + 1) * T],
                                            m8[s][:, i, :, :].rearrange("p h e -> p (h e)"), ident16)
                elif h.endswith("oT"):
                    pe.wait_ge(s_on[s], layer(g, h[0]))
                    for i in range(SPS):
                        last = pe.transpose(bank[:, i * T:(i + 1) * T], on[s][:, i, :], ident)
                elif h.endswith("wo"):
                    for i in range(SPS):
                        last = mm(bank[:, i * D:(i + 1) * D], oT[s][:, i * T:(i + 1) * T],
                                  P("wo0" if h[0] == "B" else "wo1"), start=True, stop=h[0] == "C")
                        if h[0] == "B":
                            last = mm(bank[:, i * D:(i + 1) * D], onesrow[:], bof[:], start=False, stop=True)
                elif h == "D.yT":
                    pe.wait_ge(s_y[s], g + 1)
                    for i in range(SPS):
                        last = pe.transpose(bank[:, i * T:(i + 1) * T], y[s][:, i, :], ident)
                elif h == "D.lg":
                    for i in range(SPS):
                        last = mm(bank[:, i * E1:(i + 1) * E1], yT[s][:, i * T:(i + 1) * T], P("gate"),
                                  start=True, stop=True)
                elif h == "D.cT":
                    pe.wait_ge(s_comb[s], g + 1)
                    for i in range(SPS):
                        last = pe.transpose(bank[0:E1, i * T:(i + 1) * T], comb[:, (s - NS) * SPS + i, :], ident)
                last.then_inc(s_hop[s], 1)

            def stack_rows(s, n, q, t, i, width):
                return qk[s][32 * q:32 * q + 32, n, t, i * T:i * T + width]

            def stacking(g, count, st):
                _, s, L, u = st
                n, t0 = u // 2, u % 2 * 2
                if u == 0:
                    pe.wait_ge(s_hl[s], layer(g, L))
                src = hlC[s - NS] if L == "C" else hl[s]
                b, j = count("bank", st, BANKS)
                pe.wait_ge(s_free[b], j + 1)
                for t in (t0, t0 + 1):
                    for part in range(2):
                        m = t * 4 + 2 * n + part
                        pick = H("pick")[:, m * 128:(m + 1) * 128]
                        last = mm(bk[b][:, (t - t0) * W:(t - t0 + 1) * W], pick, src[:, 2 * n + part, :],
                                  start=part == 0, stop=part == 1)
                last.then_inc(s_full[b], 1)

            def weighted(g, count, s, L, u):
                i, q = divmod(u, NQ)
                if u == 0:
                    pe.wait_ge(s_read[s], hop(g, L + ".pv"))
                    if L == "C":
                        pe.wait_ge(s_read[s - NS], read(g, "C.v"))
                p, n = exp_unit(count, s, L, u)
                pe.wait_ge(s_exp, n + 1)
                if u in LOW_DVE:
                    pe.wait_ge(s_lodve, count("low dve", ("low", s, L, u))[1] + 1)
                else:
                    pe.wait_ge(s_lopool, count("low pool", ("low", s, L, u))[1] + 1)
                nk = KEYS[L]
                v_hi, v_lo = values(s, L)
                for t in range(NT):
                    h = NQ * t + q
                    o = mb[s][:, (i * NH + h) * VW:(i * NH + h + 1) * VW]
                    high, low = (e[0:nk, p, t * T:(t + 1) * T] for e in (phi, plo))
                    mm(o, high, v_hi[0:nk, i, h, :], start=True, stop=False)
                    mm(o, high, v_lo[0:nk, i, h, :], start=False, stop=False)
                    last = mm(o, low, v_hi[0:nk, i, h, :], start=False, stop=True)
                last.then_inc(s_pv, 1)

            def scores(g, count, st, q_first):
                _, s, L, u = st
                i, q = divmod(u, NQ)
                nk = KEYS[L]
                b, j = count("bank", st, BANKS)
                pe.wait_ge(s_free[b], j + 1)
                for t in range(NT):
                    qs, ks = stack_rows(s, 0, q, t, i, T), stack_rows(s, 1, q, t, i, nk)
                    o = bk[b][:, t * nk:(t + 1) * nk] if q_first else bk[b][0:nk, t * T:(t + 1) * T]
                    last = mm(o, qs if q_first else ks, ks if q_first else qs, start=L != "D" or t == 0,
                              stop=L != "D")
                if L == "D":
                    last = mm(bk[b][:], ident16, H("maskS" if q_first else "maskST"), start=False, stop=True)
                last.then_inc(s_full[b], 1)

            def down(g, count, k):
                e, c = divmod(k, CH)
                if c == 0:
                    pe.wait_ge(s_acc, g * (E1 + 1) + e + 2)
                b, j = count("bank", ("moe", k), BANKS)
                pe.wait_ge(s_free[b], j + 2)
                for i in range(GROUP):
                    last = mm(db[:, i * D:(i + 1) * D], hT[:, k % 2, i * T:(i + 1) * T], w2f[:, k, :],
                              start=c == 0 and i == 0, stop=c == CH - 1, skip_group_check=True)
                last.then_inc(s_down, 1)

            def step(g, count, st):
                kind = st[0]
                if kind == "hop" and not st[2].endswith("pv"):
                    hop_step(g, st[1], st[2])
                elif kind == "stack":
                    stacking(g, count, st)
                elif kind == "M":
                    _, s, L, u = st
                    if u == 0:
                        for n in range(STACKINGS - BANKS, STACKINGS):
                            b, j = count("bank", ("stack", s, L, n), BANKS)
                            if b != count("bank", st, BANKS)[0]:
                                pe.wait_ge(s_free[b], j + 2)
                    scores(g, count, st, True)
                elif kind == "E":
                    _, s, L, u = st
                    if u == 0:
                        pe.wait_ge(s_max[s], layer(g, L) * 16 * MAX_DMAS)
                    scores(g, count, st, False)
                elif kind == "PV":
                    weighted(g, count, *st[1:])
                elif kind == "moe_start":
                    pe.wait_ge(s_acc, g * (E1 + 1) + 1)
                    if isinstance(g, int) and g == 0:
                        pe.wait_ge(s_moe, N_MOE * 16)
                        pe.wait_ge(s_w1lo, 1)
                    for i in range(GROUP):
                        s = NS + i // SPS
                        if i % SPS == 0:
                            pe.wait_ge(s_read[s], read(g, "D.cT"))
                        last = mm(db[:, i * D:(i + 1) * D], combT[s][:, (i % SPS) * T:(i % SPS + 1) * T], b2f[:],
                                  start=True, stop=True)
                    last.then_inc(s_accinit, 1)
                    pe.wait_ge(s_y16, NS * (g + 1))
                elif kind == "moe":
                    k = st[1]
                    b, j = count("bank", st, BANKS)
                    pe.wait_ge(s_free[b], j + 1)
                    hi, lo = (w[:, k * 128:(k + 1) * 128] for w in (w1hi, w1lo))
                    mm(bk[b][:], hi, yhi[:], start=True, stop=False)
                    mm(bk[b][:], hi, ylo[:], start=False, stop=False)
                    mm(bk[b][:], lo, yhi[:], start=False, stop=True).then_inc(s_full[b], 1)
                    if k:
                        down(g, count, k - 1)
                elif kind == "moe_end":
                    down(g, count, UNITS - 1)
                elif kind == "skip":
                    b, j = count("bank", st, BANKS)
                    pe.wait_ge(s_free[b], j + 1)
                    pe.sem_inc(s_full[b], 1)

            def ready():
                pe.wait_ge(s_const, N_CONST * 16)

            pe.wait_ge(s_first, 2 * 16)
            pe.wait_ge(s_init_dve, 1)
            pe.wait_ge(s_init_pool, 1)
            run(pe, step, ready)

        @block.scalar
        def _(act):
            def hop_step(g, s, h):
                bank = mb[s]
                if h not in ("ctxT", "A.xT", "A.s", "A.pT", "C.v", "B.xT", "B.hid", "B.lg", "B.qk", "B.v", "B.mt",
                             "C.xT", "C.mt", "C.oT", "D.xT", "D.qk", "D.v", "D.mt", "D.yT", "D.lg"):
                    return
                if h in ("B.lg", "D.lg"):
                    n = SPS * (E0 if h == "B.lg" else E1)
                    act.wait_ge(s_lsub[s], g + 1)
                    act.activation(lexp[s][:, 0:n], lsub[s][:, 0:n], ACT.Exp).then_inc(s_lexp[s], 1)
                    return
                if h == "B.qk":
                    act.wait_ge(s_qkf[s], g + 1)
                    act.activation(hl[s][:, 0:4:2, :], qkf[s][:], ACT.Copy).then_inc(s_hi[s], 1)
                    return
                act.wait_ge(s_hop[s], hop(g, h))
                if h == "A.s":
                    act.wait_ge(s_nmA[s], g + 1)
                    for i in range(SPS):
                        last = act.activation(pA[s][:, i, :], bank[:, i * NKC:(i + 1) * NKC], ACT.Exp,
                                              bias=nmA[s][:, i:i + 1], accum_out=sumA[s][:, i:i + 1])
                elif h == "ctxT":
                    last = act.activation(ctxT[s][:], bank[:, 0:SPS * NKC], ACT.Copy)
                elif h == "B.xT":
                    for i in range(SPS):
                        last = act.activation(xnT[s][:, i * T:(i + 1) * T], bank[:, i * T:(i + 1) * T], ACT.Copy,
                                              accum_out=pooled[s][:, i:i + 1])
                elif h in ("A.xT", "C.xT", "D.xT"):
                    last = act.activation(xnT[s][:], bank[:, 0:W], ACT.Copy)
                elif h == "A.pT":
                    last = act.activation(pAT[s][:], bank[0:NKC, 0:W], ACT.Copy)
                elif h == "B.hid":
                    last = act.activation(hid[s][:], bank[:, 0:SPS], ACT.Relu, bias=P("bg1"), scale=1.0 / T)
                elif h in ("B.v", "D.v", "C.v"):
                    act.activation(value_heads(values(s, h[0])[0]), bank_heads(bank, h[0]), ACT.Copy
                                   ).then_inc(s_vhi[s], 1)
                    return
                elif h.endswith("mt"):
                    last = act.activation(mT[s][:], bank[:].bitcast(F16)[:, 0:W], ACT.Copy)
                elif h == "C.oT":
                    last = act.activation(oT[s][:], bank[:, 0:W], ACT.Copy)
                elif h == "D.qk":
                    act.activation(hl[s][:, 0:4:2, :], bank[:].rearrange("p (n w) -> p n w", n=2), ACT.Copy
                                   ).then_inc(s_hi[s], 1)
                    return
                elif h == "D.yT":
                    last = act.activation(yT[s][:], bank[:, 0:W], ACT.Copy)
                last.then_inc(s_read[s], 1)

            def step(g, count, st):
                kind = st[0]
                if kind == "hop":
                    hop_step(g, st[1], st[2])
                elif kind == "stack" and st[3] not in STACK_DVE:
                    _, s, L, u = st
                    b, j = count("bank", st, BANKS)
                    act.wait_ge(s_full[b], j + 1)
                    if u < 2:
                        ins = act.activation(stack_part(s, u), bk[b][:], ACT.Copy)
                    else:
                        ins = act.activation(stack_part(s, u), bk[b][:], ACT.Identity, bias=P("ones"))
                    ins.then_inc(s_free[b], 1)
                elif kind == "E":
                    _, s, L, u = st
                    nk = KEYS[L]
                    b, j = count("bank", st, BANKS)
                    p, n = exp_unit(count, s, L, u)
                    act.wait_ge(s_full[b], j + 1)
                    act.wait_ge(s_pv, n + 1)
                    act.activation(probs[0:nk, p, :], bk[b][0:nk, :], ACT.Exp, scale=SCALE[L]
                                   ).then_inc(s_free[b], 1)
                    act.wait_ge(s_free[b], j + 2)
                    act.activation(phi[0:nk, p, :], probs[0:nk, p, :], ACT.Copy).then_inc(s_exp, 1)
                elif kind == "moe":
                    k = st[1]
                    b, j = count("bank", st, BANKS)
                    act.wait_ge(s_full[b], j + 1)
                    act.wait_ge(s_down, g * UNITS + k + 1)
                    act.activation(hT[:, k % 2, :], bk[b][:], ACT.Relu, bias=P("b1")[:, k:k + 1]
                                   ).then_inc(s_free[b], 1)

            def ready():
                act.wait_ge(s_const, N_CONST * 16)

            act.wait_ge(s_first, 2 * 16)
            act.wait_ge(s_init_dve, 1)
            run(act, step, ready)

        @block.vector
        def _(dve):
            links = {"made": 0, "before": 0, "n": 0}

            def link(ins):
                links["n"] += 1
                ins.then_inc(c_dve, 1)
                dve.wait_ge(c_dve, links["before"] + links["n"])

            def top2(g, s, bank, E, dst, bias, triL, triU):
                n = SPS * E

                def v3(t):
                    return t[:, 0:n].rearrange("p (i e) -> p i e", i=SPS)

                lg3, sub3, exp3 = v3(lg[s]), v3(lsub[s]), v3(lexp[s])
                pr4 = pair[s][:, 0:n * E].rearrange("p (i e f) -> p i e f", i=SPS, e=E)
                src = bank[:, 0:n].rearrange("p (i e) -> p i e", i=SPS)
                if bias is not None:
                    ins = dve.tensor_tensor(lg3, src, bias.unsqueeze(1).to_broadcast((128, SPS, E)), ALU.add)
                else:
                    ins = dve.tensor_copy(lg3, src)
                ins.then_inc(s_read[s], 1)
                dve.wait_ge(s_read[s], read(g, "B.lg" if E == E0 else "D.lg"))
                link(dve.tensor_reduce(lmax[s][:], lg3, X_AXIS, ALU.max))
                dve.tensor_tensor(sub3, lg3, lmax[s][:].unsqueeze(2).to_broadcast((128, SPS, E)),
                                  ALU.subtract).then_inc(s_lsub[s], 1)
                for i in range(SPS):
                    ins = dve.tensor_tensor(pr4[:, i], lg3[:, i].unsqueeze(1).to_broadcast((128, E, E)),
                                            lg3[:, i].unsqueeze(2).to_broadcast((128, E, E)), ALU.subtract)
                link(ins)
                dve.scalar_tensor_tensor(out=above[s][:, 0:n * E], in0=pair[s][:, 0:n * E], scalar=0.0, in1=triU,
                                         op0=ALU.is_gt, op1=ALU.mult)
                link(dve.scalar_tensor_tensor(out=tied[s][:, 0:n * E], in0=pair[s][:, 0:n * E], scalar=0.0,
                                                 in1=triL, op0=ALU.is_ge, op1=ALU.mult))
                link(dve.tensor_tensor(pair[s][:, 0:n * E], above[s][:, 0:n * E], tied[s][:, 0:n * E], ALU.add))
                link(dve.tensor_reduce(rank[s][:, 0:n], pair[s][:, 0:n * E].rearrange("p (n f) -> p n f", f=E),
                                          X_AXIS, ALU.add))
                dve.wait_ge(s_lexp[s], g + 1)
                link(dve.scalar_tensor_tensor(out=picked[s][:, 0:n], in0=rank[s][:, 0:n], scalar=2.0,
                                                 in1=lexp[s][:, 0:n], op0=ALU.is_lt, op1=ALU.mult))
                link(dve.tensor_reduce(psumw[s][:], v3(picked[s]), X_AXIS, ALU.add))
                link(dve.reciprocal(lmax[s][:], psumw[s][:]))
                return dve.tensor_tensor(dst, v3(picked[s]), lmax[s][:].unsqueeze(2).to_broadcast((128, SPS, E)),
                                         ALU.mult)

            def rope(g, s, h, n, hi, lo):
                bank = mb[s]
                dve.wait_ge(s_hop[s], hop(g, h))

                def v3(t):
                    return t[:, 0:SPS * n].rearrange("p (i w) -> p i w", i=SPS)

                cos = P("cos")[:, 0:n].unsqueeze(1).to_broadcast((128, SPS, n))
                sin = P("sin")[:, 0:n].unsqueeze(1).to_broadcast((128, SPS, n))
                dve.tensor_tensor(v3(rope1[s]), v3(bank), cos, ALU.mult)
                dve.tensor_tensor(v3(rope2[s]), bank[:, 256:256 + SPS * n].rearrange("p (i w) -> p i w", i=SPS), sin,
                                  ALU.mult).then_inc(s_read[s], 1)
                dve.wait_ge(s_read[s], read(g, h))
                link(dve.tensor_tensor(qkf[s][:, 0, 0:SPS * n], rope1[s][:, 0:SPS * n], rope2[s][:, 0:SPS * n],
                                          ALU.add))
                link(dve.tensor_copy(hi, v3(qkf[s][:, 0, :])))
                return dve.tensor_tensor(lo, v3(qkf[s][:, 0, :]), hi, ALU.subtract)

            def split_w1():
                dve.wait_ge(s_moe, N_MOE * 16)
                dve.tensor_copy(w1hi[:], w1f[:]).then_inc(s_w1hi, 1)
                dve.wait_ge(s_w1hi, 1)
                dve.tensor_tensor(w1lo[:], w1f[:], w1hi[:], ALU.subtract).then_inc(s_w1lo, 1)

            def hop_step(g, count, s, h):
                bank = mb[s]
                halves = bank[:].rearrange("p (n w) -> p n w", n=2)
                if h == "A.s":
                    dve.wait_ge(s_hop[s], hop(g, h))
                    dve.tensor_reduce(nmA[s][:], bank[:, 0:SPS * NKC].rearrange("p (i k) -> p i k", i=SPS), X_AXIS,
                                      ALU.max, negate=True).then_inc(s_nmA[s], 1)
                elif h == "A.o":
                    dve.wait_ge(s_hop[s], hop(g, h))
                    link(dve.reciprocal(rinvA[s][:], sumA[s][:]))
                    for i in range(SPS):
                        last = dve.scalar_tensor_tensor(out=xs[s][:, i, :], in0=bank[:, i * D:(i + 1) * D],
                                                        scalar=rinvA[s][:, i:i + 1], in1=xin[s][:, i, :],
                                                        op0=ALU.mult, op1=ALU.add)
                    last.then_inc(s_read[s], 1)
                elif h == "C.k":
                    k4 = hlC[s][:, 2:4, :].rearrange("p n (i w) -> p n i w", i=SPS)
                    link(rope(g, s, h, NKC, k4[:, 0, :, 0:NKC], k4[:, 1, :, 0:NKC]))
                elif h == "C.q":
                    q4 = hlC[s - NS][:, 0:2, :].rearrange("p n (i w) -> p n i w", i=SPS)
                    rope(g, s, h, T, q4[:, 0], q4[:, 1]).then_inc(s_hl[s], 1)
                elif h == "B.hid":
                    dve.wait_ge(s_read[s], read(g, h))
                    dve.tensor_copy(hidw[s][:], hid[s][:].unsqueeze(2).to_broadcast((128, SPS, 128))
                                    ).then_inc(s_hidw[s], 1)
                elif h == "B.lg":
                    dve.wait_ge(s_hop[s], hop(g, h))
                    link(top2(g, s, bank, E0, gw[s][:], R("bg2"), P("triL0"), P("triU0")))
                    w0 = P("w0").rearrange("p (e w) -> p e w", e=E0)
                    for e in range(E0):
                        for i in range(SPS):
                            if e == 0:
                                ins = dve.tensor_scalar(wc[s][:, i, :], w0[:, e, :], gw[s][:, i, e:e + 1], None,
                                                        ALU.mult)
                            else:
                                ins = dve.scalar_tensor_tensor(out=wc[s][:, i, :], in0=w0[:, e, :],
                                                               scalar=gw[s][:, i, e:e + 1], in1=wc[s][:, i, :],
                                                               op0=ALU.mult, op1=ALU.add)
                        if e < E0 - 1:
                            link(ins)
                    ins.then_inc(s_wc[s], 1)
                    b0 = P("b0").rearrange("p (n e) -> p n e", n=3)
                    for n in range(3):
                        ins = dve.tensor_tensor(bmix[s][:, n], b0[:, n, :].unsqueeze(1).to_broadcast((128, SPS, E0)),
                                                gw[s][:], ALU.mult)
                    link(ins)
                    link(dve.tensor_reduce(bqkv[s][:], bmix[s][:].rearrange("p n i e -> p (n i) e"), X_AXIS,
                                              ALU.add))
                elif h == "B.qk":
                    dve.wait_ge(s_hop[s], hop(g, h))
                    dve.tensor_tensor(qkf[s][:].rearrange("p n (i w) -> p (n i) w", i=SPS),
                                      bank[:].rearrange("p (m w) -> p m w", w=T),
                                      bqkv[s][:, 0:2 * SPS].unsqueeze(2).to_broadcast((128, 2 * SPS, T)), ALU.add
                                      ).then_inc(s_qkf[s], 1)
                    dve.wait_ge(s_qkf[s], g + 1)
                    dve.sem_inc(s_read[s], 1)
                    dve.wait_ge(s_hi[s], g + 1)
                    dve.tensor_tensor(hl[s][:, 1:4:2, :], qkf[s][:], hl[s][:, 0:4:2, :], ALU.subtract
                                      ).then_inc(s_hl[s], 1)
                elif h == "D.qk":
                    dve.wait_ge(s_hi[s], g + 1)
                    link(dve.tensor_tensor(hl[s][:, 1:4:2, :], halves, hl[s][:, 0:4:2, :], ALU.subtract))
                    dve.sem_inc(s_hl[s], 1)
                    dve.sem_inc(s_read[s], 1)
                elif h in ("C.v", "B.v", "D.v"):
                    if ("hop", s, h) == SPLIT and isinstance(g, int) and g == 0:
                        split_w1()
                    dve.wait_ge(s_vhi[s], g + 1 if h == "D.v" else 2 * g + 1 + ("B.v", "C.v").index(h))
                    high, low = values(s, h[0])
                    dve.tensor_tensor(value_heads(low), bank_heads(bank, h[0]), value_heads(high), ALU.subtract
                                      ).then_inc(s_read[s], 1)
                elif h.endswith("pv"):
                    dve.wait_ge(s_pv, exp_unit(count, s, h[0], UPP - 1)[1] + 1 + RING)
                    o3 = bank[:, 0:SPS * NH * VW].rearrange("p (n e) -> p n e", e=VW)
                    link(dve.reciprocal(rden[s][:].unsqueeze(2), o3[:, :, HD:VW]))
                    dve.tensor_tensor(on[s][:].rearrange("p i (h e) -> p (i h) e", e=HD), o3[:, :, 0:HD],
                                      rden[s][:].unsqueeze(2).to_broadcast((128, SPS * NH, HD)), ALU.mult
                                      ).then_inc(s_on[s], 1)
                    dve.wait_ge(s_on[s], layer(g, h[0]))
                    dve.sem_inc(s_hop[s], 1)
                    dve.sem_inc(s_read[s], 1)
                elif h == "B.oT":
                    dve.wait_ge(s_hop[s], hop(g, h))
                    for i in range(SPS):
                        last = dve.tensor_scalar(oT[s][:, i * T:(i + 1) * T], bank[:, i * T:(i + 1) * T],
                                                 bqkv[s][:, 2 * SPS + i:2 * SPS + i + 1], None, ALU.add)
                    last.then_inc(s_read[s], 1)
                elif h.endswith("wo"):
                    dve.wait_ge(s_hop[s], hop(g, h))
                    if h == "B.wo":
                        after(dve, s_read[s + NS], read(g - 1, "C.wo"))
                        src, dst = xs[s], xm[s]
                    else:
                        after(dve, s_base[s], g)
                        src, dst = xm[s - NS], xs[s]
                    dve.tensor_tensor(dst[:].rearrange("p i d -> p (i d)"), bank[:, 0:W],
                                      src[:].rearrange("p i d -> p (i d)"), ALU.add).then_inc(s_read[s], 1)
                elif h == "D.yT":
                    dve.wait_ge(s_read[s], read(g, h))
                    a, b = (s - NS) * W, (s - NS + 1) * W
                    link(dve.tensor_copy(yhi[:, a:b], yT[s][:]))
                    dve.tensor_tensor(ylo[:, a:b], yT[s][:], yhi[:, a:b], ALU.subtract).then_inc(s_y16, 1)
                elif h == "D.lg":
                    dve.wait_ge(s_hop[s], hop(g, h))
                    top2(g, s, bank, E1, comb[:, (s - NS) * SPS:(s - NS + 1) * SPS, :], None, P("triL1"), P("triU1")
                         ).then_inc(s_comb[s], 1)
                elif h == "D.cT":
                    dve.wait_ge(s_hop[s], hop(g, h))
                    dve.tensor_copy(combT[s][:], bank[0:E1, 0:W]).then_inc(s_read[s], 1)

            def take_up(g, e):
                dve.wait_ge(s_down, g * UNITS + (e + 1) * CH + 2)
                for i in range(GROUP):
                    last = dve.scalar_tensor_tensor(out=acc[:, i, :], in0=db[:, i * D:(i + 1) * D],
                                                    scalar=comb[:, i, e:e + 1], in1=acc[:, i, :],
                                                    op0=ALU.mult, op1=ALU.add)
                last.then_inc(s_acc, 1)
                dve.wait_ge(s_acc, g * (E1 + 1) + e + 3)

            def norm_source(s, N):
                return {"A": xin[s], "B": xs[s], "C": xm[s - NS], "D": xs[s], "D2": on[s]}[N]

            def step(g, count, st):
                kind = st[0]
                if kind == "ln1":
                    _, s, N = st
                    if N == "A":
                        dve.wait_ge(s_loaded[s], 32 * (g + 1))
                    elif N == "B":
                        dve.wait_ge(s_read[s], read(g, "A.o"))
                    elif N == "D2":
                        dve.wait_ge(s_on[s], layer(g, "D"))
                    elif N == "C":
                        dve.wait_ge(s_read[s - NS], read(g, "B.wo"))
                    else:
                        dve.wait_ge(s_read[s], read(g, "C.wo"))
                    src = norm_source(s, N)
                    for i in range(SPS):
                        ins = dve.bn_stats(stats[s][:, i, :], src[:, i, :])
                    link(ins)
                    dve.sem_inc(s_passed[0], 1)
                    for i in range(SPS):
                        ins = dve.bn_aggr(mv[s][:, i, :], stats[s][:, i, :])
                    link(ins)
                    dve.tensor_scalar(ve[s][:], mv[s][:, :, 1], EPS, None, ALU.add).then_inc(s_ve[s], 1)
                elif kind == "ln2":
                    _, s, N = st
                    dve.wait_ge(s_rstd[s], norm(g, N))
                    src = norm_source(s, N)
                    dst = {"D": xnD, "D2": z}.get(N, xn)[s]
                    for i in range(SPS):
                        last = dve.tensor_scalar(dst[:, i, :], src[:, i, :], mv[s][:, i, 0:1], rstd[s][:, i:i + 1],
                                                 ALU.subtract, ALU.mult)
                    last.then_inc(s_xn[s], 1)
                elif kind == "y":
                    s = st[1]
                    dve.wait_ge(s_xn[s], norm(g, "D2"))
                    link(dve.tensor_tensor(zg[s][:], z[s][:], R("g1").unsqueeze(1).to_broadcast((128, SPS, D)),
                                              ALU.mult))
                    dve.wait_ge(s_xnb[s], g + 1)
                    dve.tensor_tensor(y[s][:], zg[s][:], xnb[s][:], ALU.add).then_inc(s_y[s], 1)
                elif kind == "M":
                    _, s, L, u = st
                    i, q = divmod(u, NQ)
                    nk = KEYS[L]
                    b, j = count("bank", st, BANKS)
                    dve.wait_ge(s_full[b], j + 1)
                    dve.tensor_reduce(negmax[s][:, i, q:NH:NQ], bk[b][:, 0:NT * nk].rearrange(
                        "p (t k) -> p t k", t=NT), X_AXIS, ALU.max, negate=True).then_inc(s_free[b], 1)
                    if q == NQ - 1:
                        dve.wait_ge(s_free[b], j + 2)
                        link(dve.tensor_copy(m8[s][:, i, :, 0], negmax[s][:, i, :]))
                        dve.tensor_tensor(m8[s][:, i, :, 1], negmax[s][:, i, :], m8[s][:, i, :, 0], ALU.subtract
                                          ).then_inc(s_m8[s], 1)
                elif kind == "stack" and st[3] in STACK_DVE:
                    b, j = count("bank", st, BANKS)
                    dve.wait_ge(s_full[b], j + 1)
                    dve.tensor_copy(stack_part(st[1], st[3]), bk[b][:]).then_inc(s_free[b], 1)
                elif kind == "skip":
                    b, j = count("bank", st, BANKS)
                    dve.wait_ge(s_full[b], j + 1)
                    dve.sem_inc(s_free[b], 1)
                elif kind == "low" and st[3] in LOW_DVE:
                    low_part(dve, count, st, s_lodve)
                elif kind == "hop":
                    hop_step(g, count, st[1], st[2])
                elif kind == "moe_start":
                    dve.wait_ge(s_accinit, g + 1)
                    dve.tensor_copy(acc[:].rearrange("p i d -> p (i d)"), db[:]).then_inc(s_acc, 1)
                    dve.wait_ge(s_acc, g * (E1 + 1) + 2)
                elif kind == "moe":
                    k = st[1]
                    if k and k % CH == 0:
                        take_up(g, k // CH - 1)
                elif kind == "moe_end":
                    take_up(g, E1 - 1)
                    for i in range(GROUP):
                        ins = dve.bn_stats(statsF[:, i, :], acc[:, i, :])
                    link(ins)
                    dve.sem_inc(s_passed[0], 1)
                    for i in range(GROUP):
                        ins = dve.bn_aggr(mvF[:, i, :], statsF[:, i, :])
                    link(ins)
                    dve.tensor_scalar(veF[:], mvF[:, :, 1], EPS, None, ALU.add).then_inc(s_veF, 1)
                    dve.wait_ge(s_rstdF, g + 1)
                    for i in range(GROUP):
                        last = dve.tensor_scalar(zF[:, i, :], acc[:, i, :], mvF[:, i, 0:1], rstdF[:, i:i + 1],
                                                 ALU.subtract, ALU.mult)
                    last.then_inc(s_zF, 1)

            def begin(it):
                if isinstance(it, int) and it == NG:
                    assert links["n"] == LINKS, links
                    links["made"] += (NG - 2) * LINKS
                else:
                    links["made"] += links["n"]
                links["before"] = links["made"] if isinstance(it, int) else it * LINKS + (links["made"] - 2 * LINKS)
                links["n"] = 0

            for s in range(LANES):
                for v_hi, v_lo in (values(s, "B"),) + ((values(s, "C"),) if s < NS else ()):
                    dve.memset(v_hi[:, :, :, HD:VW], 1.0)
                    dve.memset(v_lo[:, :, :, HD:VW], 0.0)
                dve.memset(m8[s][:], 0.0)
                if s < NS:
                    dve.memset(hlC[s][:], 0.0)
            dve.memset(onesrow[:], 1.0).then_inc(s_init_dve, 1)
            dve.wait_ge(s_init_dve, 1)
            for s in range(LANES):
                dve.sem_inc(s_read[s], 1)
            for b in range(BANKS):
                dve.sem_inc(s_free[b], 1)
            dve.sem_inc(s_acc, 1)
            dve.wait_ge(s_first, 2 * 16)

            def ready():
                dve.wait_ge(s_const, N_CONST * 16)

            run(dve, step, ready, begin)

        @block.gpsimd
        def _(pool):
            pool.memset(neghalf[:], -0.5).then_inc(s_init_pool, 1)
            pool.wait_ge(s_init_pool, 1)
            pool.sem_inc(s_pv, RING)
            pool.sem_inc(s_down, 2)
            pool.sem_inc(s_store, 1)
            pool.sem_inc(s_outb, 1)
            pool.wait_ge(s_first, 2 * 16)

            def step(g, count, st):
                kind = st[0]
                if kind == "ln1":
                    _, s, N = st
                    pool.wait_ge(s_ve[s], norm(g, N))
                    pool.tensor_tensor(rstd[s][:], ve[s][:], neghalf[:, 0:SPS], ALU.pow).then_inc(s_rstd[s], 1)
                elif kind == "stack" and st[2:] == ("D", 0):
                    s = st[1]
                    pool.wait_ge(s_xn[s], norm(g, "D"))
                    pool.tensor_tensor(xnb[s][:], xnD[s][:], R("b1").unsqueeze(1).to_broadcast((128, SPS, D)),
                                       ALU.add).then_inc(s_xnb[s], 1)
                elif kind == "low" and st[3] not in LOW_DVE:
                    low_part(pool, count, st, s_lopool)
                elif kind == "y":
                    s = st[1]
                    pool.wait_ge(s_y[s], g + 1)
                    pool.wait_ge(s_read[s], read(g, "C.wo"))
                    pool.tensor_tensor(xy[s][:], xs[s][:], y[s][:], ALU.add).then_inc(c_pool, 1)
                    pool.wait_ge(c_pool, NS * g + s - NS + 1)
                    pool.wait_ge(s_outb, g + 1)
                    pool.tensor_tensor(base[s][:], xy[s][:], R("b2").unsqueeze(1).to_broadcast((128, SPS, D)),
                                       ALU.add).then_inc(s_base[s], 1)
                elif kind == "moe_end":
                    pool.wait_ge(s_veF, g + 1)
                    pool.tensor_tensor(rstdF[:], veF[:], neghalf[:], ALU.pow).then_inc(s_rstdF, 1)
                    pool.wait_ge(s_zF, g + 1)
                    pool.tensor_tensor(zgF[:], zF[:], R("g2").unsqueeze(1).to_broadcast((128, GROUP, D)),
                                       ALU.mult).then_inc(c_poolF, 1)
                    pool.wait_ge(c_poolF, g + 1)
                    pool.wait_ge(s_store, 16 * g + 1)
                    for s in range(NS):
                        pool.wait_ge(s_base[s + NS], g + 1)
                        a, b = s * SPS, (s + 1) * SPS
                        last = pool.tensor_tensor(outb[:, a:b, :], zgF[:, a:b, :], base[s + NS][:], ALU.add)
                    last.then_inc(s_outb, 1)

            run(pool, step, lambda: pool.wait_ge(s_const, N_CONST * 16))


def kernel(**inputs):
    import concourse.bacc as bacc
    from concourse.bass_utils import run_bass_kernel_spmd

    a = {n: np.asarray(v) for n, v in inputs.items()}
    f32 = np.float32

    swap = np.arange(D).reshape(NH, 2, HD // 2)[:, ::-1].reshape(D)
    inv_freq = (1.0 / (10000.0 ** (np.arange(0, HD, 2, dtype=f32) / f32(HD)))).astype(f32)
    angle = np.outer(np.arange(T, dtype=f32), inv_freq).astype(f32)
    cos = np.tile(np.cos(angle).T, (2 * NH, 1)).astype(f32)
    sin = np.concatenate([-np.sin(angle).T, np.sin(angle).T])
    sin = np.tile(sin, (NH, 1)).astype(f32)
    low = np.tri(T, dtype=bool)
    mask = np.where(low, 0.0, MASKED).astype(np.float16)
    pick = np.zeros((128, NT, 4, 128), np.float16)
    for part, places in enumerate(((0, 1), (2,), (0, 2), (1,))):
        for r in places:
            for row in range(128):
                pick[row, row // 32, part, 4 * (row % 32) + r] = 1.0
    ones = np.array([[float(p % 4 == 3 and p // 4 % HD < 2)] for p in range(128)], f32)
    half = {"ident16": np.eye(128, dtype=np.float16), "maskS": np.tile(mask, (1, NT)),
            "maskST": np.tile(mask.T, (1, NT)), "pick": pick.reshape(128, -1)}

    def tri(E, upper):
        m = np.triu(np.ones((E, E), f32), 1) if upper else np.tril(np.ones((E, E), f32), -1)
        return np.tile(m.reshape(1, -1), (128, SPS))

    w0 = np.stack([a[f"L0_ffn_W{n}"] for n in "qkv"], 2).transpose(1, 0, 2, 3).reshape(D, -1)
    b0 = np.stack([a[f"L0_ffn_b{n}"] for n in "qkv"], 0).transpose(2, 0, 1).reshape(D, -1)

    def heads(w):
        return w.transpose(1, 0, 2).reshape(D, D)

    pack = {"ident": np.eye(128, dtype=f32), "ones": ones, "w0": w0, "wg1": a["L0_ffn_Wg1"], "wo0": a["L0_ffn_Wo"],
            "wq": a["L1_xattn_Wq"].T, "wqp": a["L1_xattn_Wq"][swap].T,
            "wk": a["L1_xattn_Wk"].T, "wkp": a["L1_xattn_Wk"][swap].T,
            "wv": a["L1_xattn_Wv"].T, "wo1": a["L1_xattn_Wo"].T,
            "dq": heads(a["L1_ffn_Wq"]), "dk": heads(a["L1_ffn_Wk"]), "dv": heads(a["L1_ffn_Wv"]),
            "wg2": a["L0_ffn_Wg2"], "gate": a["L1_ffn_gate_W"], "bg1": a["L0_ffn_bg1"].reshape(-1, 1), "b0": b0,
            "b1": a["L1_ffn_b1"].reshape(UNITS, 128).T, "cos": cos, "sin": sin,
            "triL0": tri(E0, False), "triU0": tri(E0, True), "triL1": tri(E1, False), "triU1": tri(E1, True)}
    rows = {"g1": a["L1_ffn_ln1_g"], "b1": a["L1_ffn_ln1_b"], "g2": a["L1_ffn_ln2_g"], "b2": a["L1_ffn_ln2_b"],
            "bg2": a["L0_ffn_bg2"]}
    arrays = {
        "x": a["x"], "ctx": a["ctx_1024"],
        "pack": np.concatenate([pack[n] for n, _ in PACK], 1),
        "rows": np.concatenate([rows[n] for n, _ in ROWS]).reshape(1, -1),
        "half": np.concatenate([half[n] for n, _ in HALF], 1),
        "w1": a["L1_ffn_W1"].transpose(1, 0, 2).reshape(D, -1),
        "w2": a["L1_ffn_W2"].reshape(UNITS, 128, D).transpose(1, 0, 2),
        "b2": a["L1_ffn_b2"], "bo": a["L0_ffn_bo"].reshape(1, -1),
    }
    arrays = {n: np.ascontiguousarray(v) for n, v in arrays.items()}
    nc = bacc.Bacc("TRN2", target_bir_lowering=False, num_devices=1)
    args = {n: nc.dram_tensor(f"in_{n}", v.shape, mybir.dt.from_np(v.dtype), kind="ExternalInput").ap()
            for n, v in arrays.items()}
    out = nc.dram_tensor("out", (B, T, D), F32, kind="ExternalOutput").ap()
    build(nc, out=out, **args)
    r = run_bass_kernel_spmd(nc, [{f"in_{n}": v for n, v in arrays.items()}], core_ids=[0])
    return r.results[0]["out"]
```
